# Optimizing a Trainium2 kernel written in Bass

```python
import numpy as np
import jax
import jax.numpy as jnp

def _softmax(x, axis=-1):
    return jax.nn.softmax(x, axis=axis)

def _gelu(x):
    return jax.nn.gelu(x, approximate=True)

def _silu(x):
    return jax.nn.silu(x)

def _sigmoid(x):
    return jax.nn.sigmoid(x)

def _layernorm(x, axis=-1, eps=1e-05):
    m = jnp.mean(x, axis=axis, keepdims=True)
    v = jnp.var(x, axis=axis, keepdims=True)
    return (x - m) / jnp.sqrt(v + eps)

def _scatter_add(tgt, idx, src, axis=0):
    return tgt.at[idx].add(src)

def _segment_sum(src, seg, n):
    return jax.ops.segment_sum(src, seg, n)
kernel_name = 'mk_gnn_resnorm_d1_gnn_r8_4d5555'

def setup_inputs(seed: int=0):
    np.random.seed(seed)
    _w = jnp.asarray

    def _rec_inputs():
        import jax
        import jax.numpy as jnp
        _gk = jax.random.key(seed)
        x = -0.000202 + 1 * jax.random.normal(jax.random.fold_in(_gk, 1), (12500, 128), jnp.float32)
        src = jax.random.randint(jax.random.fold_in(_gk, 2), (200000,), 0, 12500, jnp.int32)
        dst = jnp.minimum((12500 * jax.random.uniform(jax.random.fold_in(_gk, 3), (200000,)) ** 2.0).astype(jnp.int32), 99999)
        _o = jnp.argsort(dst, stable=True)
        src = src[_o]
        dst = dst[_o]
        edge_type_9 = jax.random.randint(jax.random.fold_in(_gk, 12), (200000,), 0, 9, jnp.int32)
        return (x, src, dst, edge_type_9)
    x, src, dst, edge_type_9 = _rec_inputs()

    def _L0_gnn_setup():
        import jax, jax.numpy as jnp
        import numpy as np
        NUM_EDGE_TYPES = 8
        HIDDEN = 128
        N_NODES = 6250
        N_EDGES = 75000

        def _gru_cell(x, h, W_ih, W_hh, b_ih, b_hh):
            H = h.shape[-1]
            gi = x @ W_ih.T + b_ih
            gh = h @ W_hh.T + b_hh
            i_r, i_z, i_n = (gi[:, :H], gi[:, H:2 * H], gi[:, 2 * H:])
            h_r, h_z, h_n = (gh[:, :H], gh[:, H:2 * H], gh[:, 2 * H:])
            r = jax.nn.sigmoid(i_r + h_r)
            z = jax.nn.sigmoid(i_z + h_z)
            n = jnp.tanh(i_n + r * h_n)
            return (1.0 - z) * n + z * h
        key = jax.random.key(seed)
        ks = jax.random.split(key, 10)
        H = HIDDEN
        h = jax.random.normal(ks[0], (N_NODES, H), dtype=jnp.float32)
        edge_index = jax.random.randint(ks[1], (2, N_EDGES), 0, N_NODES, dtype=jnp.int32)
        edge_type = jax.random.randint(ks[2], (N_EDGES,), 0, NUM_EDGE_TYPES + 1, dtype=jnp.int32)
        s = 1.0 / np.sqrt(H)
        W_msg = jax.random.uniform(ks[3], (H, H), jnp.float32, -s, s)
        b_msg = jax.random.uniform(ks[4], (H,), jnp.float32, -s, s)
        edge_embed = jax.random.normal(ks[5], (NUM_EDGE_TYPES + 1, H), dtype=jnp.float32)
        W_ih = jax.random.uniform(ks[6], (3 * H, H), jnp.float32, -s, s)
        W_hh = jax.random.uniform(ks[7], (3 * H, H), jnp.float32, -s, s)
        b_ih = jax.random.uniform(ks[8], (3 * H,), jnp.float32, -s, s)
        b_hh = jax.random.uniform(ks[9], (3 * H,), jnp.float32, -s, s)
        return {'h': h, 'edge_index': edge_index, 'edge_type': edge_type, 'num_nodes': N_NODES, 'W_msg': W_msg, 'b_msg': b_msg, 'edge_embed': edge_embed, 'W_ih': W_ih, 'W_hh': W_hh, 'b_ih': b_ih, 'b_hh': b_hh}
    _L0_gnn_all = _L0_gnn_setup()
    _L0_gnn_in = {k: v for k, v in _L0_gnn_all.items() if k in ('W_msg', 'b_msg', 'edge_embed', 'W_ih', 'W_hh', 'b_ih', 'b_hh')}
    del _L0_gnn_all
    return {'x': x, 'src': src, 'dst': dst, 'edge_type_9': edge_type_9, 'L0_gnn_W_msg': _L0_gnn_in['W_msg'], 'L0_gnn_b_msg': _L0_gnn_in['b_msg'], 'L0_gnn_edge_embed': _L0_gnn_in['edge_embed'], 'L0_gnn_W_ih': _L0_gnn_in['W_ih'], 'L0_gnn_W_hh': _L0_gnn_in['W_hh'], 'L0_gnn_b_ih': _L0_gnn_in['b_ih'], 'L0_gnn_b_hh': _L0_gnn_in['b_hh']}

def reference(x, src, dst, edge_type_9, L0_gnn_W_msg, L0_gnn_b_msg, L0_gnn_edge_embed, L0_gnn_W_ih, L0_gnn_W_hh, L0_gnn_b_ih, L0_gnn_b_hh):
    import jax
    import jax.numpy as jnp

    def _L0_gnn_ref(h, edge_index, edge_type, num_nodes, W_msg, b_msg, edge_embed, W_ih, W_hh, b_ih, b_hh):
        import jax, jax.numpy as jnp
        import numpy as np
        NUM_EDGE_TYPES = 8
        HIDDEN = 128
        N_NODES = 6250
        N_EDGES = 75000

        def _gru_cell(x, h, W_ih, W_hh, b_ih, b_hh):
            H = h.shape[-1]
            gi = x @ W_ih.T + b_ih
            gh = h @ W_hh.T + b_hh
            i_r, i_z, i_n = (gi[:, :H], gi[:, H:2 * H], gi[:, 2 * H:])
            h_r, h_z, h_n = (gh[:, :H], gh[:, H:2 * H], gh[:, 2 * H:])
            r = jax.nn.sigmoid(i_r + h_r)
            z = jax.nn.sigmoid(i_z + h_z)
            n = jnp.tanh(i_n + r * h_n)
            return (1.0 - z) * n + z * h
        src = edge_index[0]
        dst = edge_index[1]
        src_h = h[src] @ W_msg.T + b_msg
        emb = edge_embed[jnp.clip(edge_type, 0, NUM_EDGE_TYPES)]
        msg = src_h + emb
        messages = jax.ops.segment_sum(msg, dst, num_segments=num_nodes)
        h_new = _gru_cell(messages, h[:num_nodes], W_ih, W_hh, b_ih, b_hh)
        result = jnp.zeros_like(h).at[:num_nodes].set(h_new)
        return result
    edge_index = jnp.stack([src, dst])
    x = _layernorm(x + _L0_gnn_ref(x, edge_index, edge_type_9, 12500, L0_gnn_W_msg, L0_gnn_b_msg, L0_gnn_edge_embed, L0_gnn_W_ih, L0_gnn_W_hh, L0_gnn_b_ih, L0_gnn_b_hh), axis=-1)
    return x

_drawn_inputs = setup_inputs


def setup_inputs(seed=0):
    import zlib

    import numpy as np

    out = dict(_drawn_inputs(seed))
    spreads = {}
    factors = {'L0_gnn_b_ih': 5.821, 'L0_gnn_b_hh': 7.52}
    for name, (base, spread) in spreads.items():
        noise = np.random.default_rng([zlib.crc32(name.encode()), seed]).standard_normal(out[name].shape)
        drawn = base * np.exp(spread * noise) if base else spread * noise
        out[name] = jnp.asarray(drawn.astype(out[name].dtype))
    for name, factor in factors.items():
        out[name] = (out[name] * factor).astype(out[name].dtype)
    return out
```

```python
import concourse.bass as bass
from concourse import mybir
from contextlib import ExitStack

N, H, E, NT = 12500, 128, 200000, 9
P = 128
G = 4
TILES = 1564
GROUPS = TILES // G
EP = TILES * P
W = 96
RING = 23
ROUNDS = TILES // RING
DUMP = N + W
ACC = N + W + 4
GP = 512
BN = 512
BLOCKS = [(b, min(BN, N - b)) for b in range(0, N, BN)]
EPS = 1e-5

F32 = mybir.dt.float32
I32 = mybir.dt.int32
ALU = mybir.AluOpType
ACT = mybir.ActivationFunctionType
AX = mybir.AxisListType.X
ET = mybir.EngineType


def gnn_kernel(nc, x, xT, srcT, dstT, dstG, dstE, typT, wmT, bmsg, emb, wihT, whhT, bih, bhh, out):
    ctx = ExitStack()
    with ctx:
        def sb(name, shape, dt=F32):
            return ctx.enter_context(nc.sbuf_tensor(name, shape, dt))

        def pb(name):
            return ctx.enter_context(nc.psum_tensor(name, [P, 512], F32))

        def sem(name):
            return ctx.enter_context(nc.semaphore(name))

        acc = sb("acc", [P, 2, ACC])
        idx = sb("idx", [P, TILES], I32)
        rel = sb("rel", [P, GROUPS, G])
        dstI = sb("dstI", [P, GROUPS, G], I32)
        typI = sb("typI", [P, TILES], I32)
        typF = sb("typF", [P, GROUPS, G])
        gI = sb("gI", [P, 4, 512], I32)
        gF = sb("gF", [P, 4, 512])
        mn = sb("mn", [P, 4])
        mx = sb("mx", [P, 4])
        viol = sb("viol", [P, 4])
        vsum = sb("vsum", [P, 1])
        mnI = sb("mnI", [P, 4], I32)
        flag = sb("flag", [1, 1], I32)
        baseI = sb("baseI", [P, GP], I32)
        baseF = sb("baseF", [P, GP])
        ones = sb("ones", [P, 1])
        iotaW = sb("iotaW", [P, W])
        iotaT = sb("iotaT", [P, NT])
        ident = sb("ident", [P, P])
        xg = sb("xg", [P, RING, H])
        oh = sb("oh", [P, 2, G, W])
        toh = sb("toh", [P, 2, G, NT])
        wm = sb("wm", [P, H])
        em = sb("em", [NT, H])
        bmb = sb("bmb", [NT, H])
        emb2 = sb("emb2", [NT, H])
        wih = sb("wih", [P, 3 * H])
        whh = sb("whh", [P, 3 * H])
        bi = sb("bi", [P, 3])
        bh = sb("bh", [P, 3])
        bs = sb("bs", [P, 2])
        xb = sb("xb", [P, 3, BN])
        msg = sb("msg", [P, 2, BN])
        rz = sb("rz", [P, 2, 2, BN])
        gM = rz[:, :, :, :].rearrange("p a b n -> p (a b) n")
        tn = sb("tn", [P, 3, BN])
        yT = sb("yT", [P, 2, BN])
        st = sb("st", [P, 4, 6])
        mv = sb("mv", [P, 4, 2])
        rs = sb("rs", [P, 4])
        sd = sb("sd", [P, 4])
        spare = sb("spare", [P, 1])
        eps = sb("eps", [P, 1])
        yo = sb("yo", [P, 2, 4, H])

        base_d = nc.dram_tensor("base_scratch", (GP,), I32, kind="Internal").ap()

        psg = [pb("psg0"), pb("psg1")]
        psm, psr, psz, psi, psh, pst = [pb(n) for n in ("psm", "psr", "psz", "psi", "psh", "pst")]

        def plane(b, w):
            return psg[b][:, 0:2 * w].rearrange("p (a w) -> p a w", a=2)

        s_idx = sem("s_idx")
        s_gl = sem("s_gl")
        s_dl = sem("s_dl")
        s_tl = sem("s_tl")
        s_w = sem("s_w")
        s_io = sem("s_io")
        s_id = sem("s_id")
        s_d = sem("s_d")
        s_mn = sem("s_mn")
        s_bd = sem("s_bd")
        s_bb = sem("s_bb")
        s_vi = sem("s_vi")
        s_vp = sem("s_vp")
        s_fl = sem("s_fl")
        s_g = [sem(f"s_g{i}") for i in range(RING)]
        s_used = sem("s_used")
        s_oh = sem("s_oh")
        s_grp = sem("s_grp")
        s_acc = sem("s_acc")
        s_toh = sem("s_toh")
        s_tr = sem("s_tr")
        s_sl = sem("s_sl")
        s_main = sem("s_main")
        s_x = [sem(f"s_x{i}") for i in range(3)]
        s_pm = sem("s_pm")
        s_ms = sem("s_ms")
        s_pg = sem("s_pg")
        s_rz = sem("s_rz")
        s_t2 = sem("s_t2")
        s_n = sem("s_n")
        s_dv = sem("s_dv")
        s_y = sem("s_y")
        s_pt = sem("s_pt")
        s_ln = sem("s_ln")
        s_mv = sem("s_mv")
        s_sd = sem("s_sd")
        s_o = [sem(f"s_o{i}") for i in range(2)]

        block = ctx.enter_context(nc.Block())

        def store(sp, b):
            n0, n = BLOCKS[b]
            q = n // 4
            sp.wait_ge(s_ln, b + 1)
            sp.dma_start(out[n0:n0 + n, :].rearrange("(p s) h -> p (s h)", s=4),
                         yo[0:q, b % 2, :, :].rearrange("p s h -> p (s h)")).then_inc(s_o[b % 2], 16)

        @block.sync
        def _(sp):
            sp.dma_start(idx[:, :], srcT).then_inc(s_idx, 16)
            sp.dma_start(gI[:, :, :], dstG).then_inc(s_gl, 16)
            sp.dma_start(dstI[:, :, :], dstT).then_inc(s_dl, 16)
            sp.dma_start(typI[:, :], typT).then_inc(s_tl, 16)
            sp.dma_start(wm[:, :], wmT).then_inc(s_w, 16)
            sp.dma_start(em[:, :], emb).then_inc(s_w, 16)
            sp.dma_start(bmb[:, :], bmsg.partition_broadcast(NT)).then_inc(s_w, 16)
            sp.dma_start(wih[:, :], wihT).then_inc(s_w, 16)
            sp.dma_start(whh[:, :], whhT).then_inc(s_w, 16)
            sp.dma_start(bi[:, :], bih).then_inc(s_w, 16)
            sp.dma_start(bh[:, :], bhh).then_inc(s_w, 16)
            sp.wait_ge(s_mn, 1)
            sp.dma_start(base_d.rearrange("(p j) -> p j", j=4), mnI[:, :]).then_inc(s_bd, 16)
            sp.wait_ge(s_bd, 16)
            sp.dma_start(baseI[:, :], base_d.partition_broadcast(P)).then_inc(s_bb, 16)
            for b, (n0, n) in enumerate(BLOCKS):
                if b >= 3:
                    sp.wait_ge(s_y, b - 2)
                    sp.wait_ge(s_pg, 4 * (b - 2))
                sp.dma_start(xb[:, b % 3, 0:n], xT[:, n0:n0 + n]).then_inc(s_x[b % 3], 16)
                if b >= 2:
                    store(sp, b - 2)
            for b in range(len(BLOCKS) - 2, len(BLOCKS)):
                store(sp, b)
            for i in range(2):
                sp.wait_ge(s_o[i], 16 * len(BLOCKS[i::2]))

        @block.gpsimd
        def _(pool):
            pool.iota(iotaW[:, :], [[1, W]], base=0, channel_multiplier=0,
                      allow_small_or_imprecise_dtypes=True).then_inc(s_io, 1)
            pool.iota(iotaT[:, :], [[1, NT]], base=0, channel_multiplier=0,
                      allow_small_or_imprecise_dtypes=True).then_inc(s_io, 1)
            pool.memset(ident[:, :], 0.0).then_inc(s_id, 1)
            pool.wait_ge(s_id, 1)
            pool.affine_select(out=ident[:, :], in_=ident[:, :], compare_op=ALU.not_equal, fill=1.0,
                               base=0, pattern=[[-1, P]], channel_multiplier=1).then_inc(s_id, 1)
            pool.wait_ge(s_idx, 16)
            for t in range(TILES):
                if t >= RING:
                    pool.wait_ge(s_used, t - RING + 1)
                pool.indirect_dma_start(
                    out=xg[:, t % RING, :], out_offset=None, in_=x,
                    in_offset=bass.IndirectOffsetOnAxis(ap=idx[:, t:t + 1], axis=0),
                ).then_inc(s_g[t % RING], 16)

        @block.vector
        def _(v):
            cnt = [0]

            def step(ins):
                cnt[0] += 1
                ins.then_inc(s_d, 1)
                return cnt[0]

            def link(ins):
                v.wait_ge(s_d, step(ins))

            v.wait_ge(s_gl, 16)
            link(v.tensor_copy(gF[:, :, :], gI[:, :, :]))
            link(v.tensor_scalar(gM[:, :, :], gF[:, :, :], 0.0, 65536.0, ALU.is_lt, ALU.mult))
            link(v.tensor_tensor(gM[:, :, :], gM[:, :, :], gF[:, :, :], ALU.add))
            link(v.tensor_reduce(mn[:, :], gM[:, :, :], AX, ALU.min))
            v.tensor_copy(mnI[:, :], mn[:, :]).then_inc(s_mn, 1)
            link(v.tensor_reduce(mx[:, :], gF[:, :, :], AX, ALU.max))
            link(v.tensor_tensor(viol[:, :], mx[:, :], mn[:, :], ALU.subtract))
            link(v.tensor_scalar(viol[:, :], viol[:, :], float(W), None, ALU.is_ge))
            link(v.tensor_reduce(vsum[:, :], viol[:, :], AX, ALU.add))
            v.memset(ones[:, :], 1.0).then_inc(s_vi, 1)
            v.memset(eps[:, :], EPS)
            v.memset(acc[:, 0, :], 0.0)
            link(v.memset(acc[:, 1, :], 0.0))
            v.wait_ge(s_vp, 1)
            v.tensor_copy(flag[:, :], psm[0:1, 0:1]).then_inc(s_fl, 1)
            v.memset(psg[0][:, :], 0.0)
            link(v.memset(psg[1][:, :], 0.0))
            v.wait_ge(s_tl, 16)
            link(v.tensor_copy(typF[:, :, :].rearrange("p g t -> p (g t)"), typI[:, :]))
            v.wait_ge(s_w, 16 * 7)
            link(v.tensor_tensor(emb2[:, :], em[:, :], bmb[:, :], ALU.add))
            link(v.tensor_tensor(bs[:, :], bi[:, 0:2], bh[:, 0:2], ALU.add))
            v.wait_ge(s_dl, 16)
            link(v.tensor_copy(rel[:, :, :], dstI[:, :, :]))
            v.wait_ge(s_bb, 16)
            link(v.tensor_copy(baseF[:, :], baseI[:, :]))
            link(v.tensor_tensor(rel[:, :, :], rel[:, :, :],
                                 baseF[:, 0:GROUPS].unsqueeze(2).to_broadcast([P, GROUPS, G]), ALU.subtract))
            v.wait_ge(s_io, 2)
            v.wait_ge(s_fl, 1)
            bad = nc.values_load(flag[0:1, 0:1], engines=[ET.DVE], min_val=0, max_val=P * 4,
                                 skip_runtime_bounds_check_because="a count of rows with a violation")

            with v.If(bad == 0):
                bases = {}

                def one_hot(g):
                    b = g % 2
                    if g >= 2:
                        v.wait_ge(s_grp, g - 1)
                    v.tensor_tensor(oh[:, b, :, :], rel[:, g, :].unsqueeze(2).to_broadcast([P, G, W]),
                                    iotaW[:, :].unsqueeze(1).to_broadcast([P, G, W]), ALU.is_equal)
                    v.tensor_tensor(toh[:, b, :, :], typF[:, g, :].unsqueeze(2).to_broadcast([P, G, NT]),
                                    iotaT[:, :].unsqueeze(1).to_broadcast([P, G, NT]),
                                    ALU.is_equal).then_inc(s_oh, 1)

                def accumulate(g):
                    if g % 4 == 0:
                        k = min(4, GROUPS - g)
                        _, vals = nc.values_load_multi_w_load_instructions(
                            baseI[0:1, g:g + k], engines=[ET.DVE], min_val=0, max_val=N - 1,
                            skip_runtime_bounds_check_because="the least destination of a group is a node")
                        for j, q in enumerate(vals):
                            bases[g + j] = q
                    d = acc[:, :, bass.ds(bases[g], W)]
                    v.wait_ge(s_grp, g + 1)
                    if g:
                        v.wait_ge(s_acc, g)
                    v.tensor_tensor(d, d, plane(g % 2, W), ALU.add).then_inc(s_acc, 1)

                for g in range(GROUPS):
                    one_hot(g)
                    if g:
                        accumulate(g - 1)
                accumulate(GROUPS - 1)
            with v.Else():
                with v.Fori(0, ROUNDS) as i:
                    for s in range(RING):
                        t = i * RING + s
                        b = s % 2
                        v.wait_ge(s_tr, t)
                        v.tensor_tensor(toh[:, 0, 0, :],
                                        typF[:, :, :].rearrange("p g t -> p (g t)")[:, bass.ds(t, 1)].to_broadcast([P, NT]),
                                        iotaT[:, :], ALU.is_equal).then_inc(s_toh, 1)
                        v.wait_ge(s_tr, t + 1)
                        v.memset(spare[:, :], 0.0)
                        with v.Fori(0, P) as e:
                            d = nc.values_load(dstE[0:1, bass.ds(t * P + e, 1)], engines=[ET.DVE],
                                               min_val=0, max_val=DUMP,
                                               skip_runtime_bounds_check_because="a destination is a node")
                            q = acc[:, :, bass.ds(d, 1)]
                            v.tensor_tensor(q, q, plane(0, P)[:, :, bass.ds(e, 1)], ALU.add)
                            v.drain()
                        v.drain().then_inc(s_sl, 1)
            v.drain().then_inc(s_main, 1)

            def gates(b):
                n0, n = BLOCKS[b]
                t = tn[:, :, 0:n]
                v.wait_ge(s_rz, 2 * b + 1)
                v.wait_ge(s_pg, 4 * b + 4)
                if b:
                    v.wait_ge(s_y, b)
                link(v.scalar_tensor_tensor(out=t[:, 0, :], in0=psh[:, 0:n], scalar=bh[:, 2:3],
                                            in1=rz[:, b % 2, 0, 0:n], op0=ALU.add, op1=ALU.mult))
                v.tensor_tensor(t[:, 1, :], t[:, 0, :], psi[:, 0:n], ALU.add).then_inc(s_t2, 1)
                v.wait_ge(s_n, b + 1)
                v.wait_ge(s_rz, 2 * b + 2)
                xx = xb[:, b % 3, 0:n]
                link(v.tensor_tensor(t[:, 0, :], xx, t[:, 2, :], ALU.subtract))
                link(v.tensor_tensor(t[:, 0, :], t[:, 0, :], rz[:, b % 2, 1, 0:n], ALU.mult))
                link(v.tensor_tensor(t[:, 1, :], xx, t[:, 2, :], ALU.add))
                if b >= 2:
                    v.wait_ge(s_pt, b - 1)
                v.tensor_tensor(yT[:, b % 2, 0:n], t[:, 0, :], t[:, 1, :], ALU.add).then_inc(s_y, 1)

            def norm(b):
                n = BLOCKS[b][1]
                q = n // 4
                v.wait_ge(s_pt, b + 1)
                if b >= 2:
                    v.wait_ge(s_o[b % 2], 16 * (b // 2))
                for s in range(4):
                    ins = v.bn_stats(st[0:q, s, :], pst[0:q, s * H:(s + 1) * H])
                link(ins)
                for s in range(4):
                    ins = v.bn_aggr(mv[0:q, s, :], st[0:q, s, :])
                ins.then_inc(s_mv, 1)
                v.wait_ge(s_sd, b + 1)
                link(v.reciprocal(rs[0:q, :], sd[0:q, :]))
                for s in range(4):
                    ins = v.tensor_scalar(yo[0:q, b % 2, s, :], pst[0:q, s * H:(s + 1) * H], mv[0:q, s, 0:1],
                                          rs[0:q, s:s + 1], ALU.subtract, ALU.mult)
                ins.then_inc(s_ln, 1)
                v.wait_ge(s_ln, b + 1)

            for b in range(len(BLOCKS)):
                gates(b)
                if b:
                    norm(b - 1)
            norm(len(BLOCKS) - 1)

        @block.tensor
        def _(pe):
            pe.wait_ge(s_vi, 1)
            pe.matmul(psm[0:1, 0:1], ones[:, :], vsum[:, :], start=True, stop=True).then_inc(s_vp, 1)
            pe.wait_ge(s_fl, 1)
            bad = nc.values_load(flag[0:1, 0:1], engines=[ET.PE], min_val=0, max_val=P * 4,
                                 skip_runtime_bounds_check_because="a count of rows with a violation")
            with pe.If(bad == 0):
                for g in range(GROUPS):
                    b = g % 2
                    pe.wait_ge(s_oh, g + 1)
                    if g >= 2:
                        pe.wait_ge(s_acc, g - 1)
                    q = plane(b, W)
                    for j in range(G):
                        t = g * G + j
                        pe.wait_ge(s_g[t % RING], 16 * (t // RING + 1))
                        pe.matmul(q[:, 0, :], xg[:, t % RING, :], oh[:, b, j, :],
                                  start=(j == 0), stop=(j == G - 1), skip_group_check=True).then_inc(s_used, 1)
                        ins = pe.matmul(q[0:NT, 1, :], toh[:, b, j, :], oh[:, b, j, :],
                                        start=False, stop=(j == G - 1), skip_group_check=True)
                    ins.then_inc(s_grp, 1)
            with pe.Else():
                pe.wait_ge(s_id, 2)
                with pe.Fori(0, ROUNDS) as i:
                    for s in range(RING):
                        t = i * RING + s
                        pe.wait_ge(s_g[s], (i + 1) * 16)
                        pe.wait_ge(s_toh, t + 1)
                        pe.wait_ge(s_sl, t)
                        q = plane(0, P)
                        pe.transpose(q[:, 0, :], xg[:, s, :], ident[:, :]).then_inc(s_used, 1)
                        pe.transpose(q[0:NT, 1, :], toh[:, 0, 0, :], ident[:, :]).then_inc(s_tr, 1)
            pe.wait_ge(s_id, 2)
            pe.wait_ge(s_main, 1)

            def turn(b):
                n = BLOCKS[b][1]
                q = n // 4
                pe.wait_ge(s_y, b + 1)
                if b:
                    pe.wait_ge(s_ln, b)
                yv = yT[:, b % 2, 0:n].rearrange("f (p s) -> f s p", s=4)
                for s in range(4):
                    ins = pe.transpose(pst[0:q, s * H:(s + 1) * H], yv[:, s, :], ident[:, :])
                ins.then_inc(s_pt, 1)

            for b, (n0, n) in enumerate(BLOCKS):
                a = acc[:, 0, n0:n0 + n]
                xx = xb[:, b % 3, 0:n]
                if b:
                    pe.wait_ge(s_ms, b)
                pe.matmul(psm[:, 0:n], wm[:, :], a, start=True, stop=False)
                pe.matmul(psm[:, 0:n], emb2[:, :], acc[0:NT, 1, n0:n0 + n], start=False,
                          stop=True).then_inc(s_pm, 1)
                pe.wait_ge(s_x[b % 3], 16 * (b // 3 + 1))
                if b:
                    pe.wait_ge(s_rz, 2 * b)
                pe.matmul(psr[:, 0:n], whh[:, 0:H], xx, start=True, stop=False, skip_group_check=True)
                pe.matmul(psz[:, 0:n], whh[:, H:2 * H], xx, start=True, stop=False, skip_group_check=True)
                if b:
                    pe.wait_ge(s_t2, b)
                pe.matmul(psh[:, 0:n], whh[:, 2 * H:3 * H], xx, start=True, stop=True).then_inc(s_pg, 1)
                pe.wait_ge(s_ms, b + 1)
                m = msg[:, b % 2, 0:n]
                pe.matmul(psr[:, 0:n], wih[:, 0:H], m, start=False, stop=True,
                          skip_group_check=True).then_inc(s_pg, 1)
                pe.matmul(psi[:, 0:n], wih[:, 2 * H:3 * H], m, start=True, stop=True).then_inc(s_pg, 1)
                pe.matmul(psz[:, 0:n], wih[:, H:2 * H], m, start=False, stop=True,
                          skip_group_check=True).then_inc(s_pg, 1)
                if b:
                    turn(b - 1)
            turn(len(BLOCKS) - 1)

        @block.scalar
        def _(act):
            def deviation(b):
                q = BLOCKS[b][1] // 4
                act.wait_ge(s_mv, b + 1)
                if b:
                    act.wait_ge(s_ln, b)
                act.activation(sd[0:q, :], mv[0:q, :, 1], ACT.Sqrt, bias=eps[0:q, 0:1]).then_inc(s_sd, 1)

            for b, (n0, n) in enumerate(BLOCKS):
                act.wait_ge(s_pm, b + 1)
                if b >= 2:
                    act.wait_ge(s_pg, 4 * (b - 1))
                act.copy(msg[:, b % 2, 0:n], psm[:, 0:n]).then_inc(s_ms, 1)
                act.wait_ge(s_pg, 4 * b + 2)
                if b >= 2:
                    act.wait_ge(s_y, b - 1)
                act.activation(rz[:, b % 2, 0, 0:n], psr[:, 0:n], ACT.Sigmoid, bias=bs[:, 0:1]).then_inc(s_rz, 1)
                act.wait_ge(s_pg, 4 * b + 4)
                act.activation(rz[:, b % 2, 1, 0:n], psz[:, 0:n], ACT.Sigmoid, bias=bs[:, 1:2]).then_inc(s_rz, 1)
                act.wait_ge(s_t2, b + 1)
                if b:
                    act.wait_ge(s_y, b)
                act.activation(tn[:, 2, 0:n], tn[:, 1, 0:n], ACT.Tanh, bias=bi[:, 2:3]).then_inc(s_n, 1)
                if b:
                    deviation(b - 1)
            deviation(len(BLOCKS) - 1)


def kernel(x, src, dst, edge_type_9, L0_gnn_W_msg, L0_gnn_b_msg, L0_gnn_edge_embed, L0_gnn_W_ih,
           L0_gnn_W_hh, L0_gnn_b_ih, L0_gnn_b_hh):
    import numpy as np
    import concourse.bacc as bacc
    from concourse.bass_utils import run_bass_kernel_spmd

    def lay(a):
        return np.ascontiguousarray(a)

    def padded(a, n, fill):
        a = np.asarray(a)
        return np.concatenate([a, np.full(n - a.shape[0], fill, a.dtype)])

    def by_tile(a, fill):
        return lay(padded(a, EP, fill).reshape(TILES, P).T)

    x = np.asarray(x)
    arrays = {
        "x": lay(x),
        "xT": lay(x.T),
        "srcT": by_tile(src, 0),
        "dstT": by_tile(dst, -1).reshape(P, GROUPS, G),
        "dstG": padded(dst, GP * G * P, -1).reshape(P, 4, 512),
        "dstE": padded(dst, EP, DUMP).reshape(1, EP),
        "typT": by_tile(edge_type_9, 0),
        "wmT": lay(np.asarray(L0_gnn_W_msg).T),
        "bmsg": lay(np.asarray(L0_gnn_b_msg)),
        "emb": lay(np.asarray(L0_gnn_edge_embed)),
        "wihT": lay(np.asarray(L0_gnn_W_ih).T),
        "whhT": lay(np.asarray(L0_gnn_W_hh).T),
        "bih": lay(np.asarray(L0_gnn_b_ih).reshape(3, H).T),
        "bhh": lay(np.asarray(L0_gnn_b_hh).reshape(3, H).T),
    }
    nc = bacc.Bacc("TRN2", target_bir_lowering=False, num_devices=1)
    args = [nc.dram_tensor(f"in_{k}", a.shape, mybir.dt.from_np(a.dtype), kind="ExternalInput").ap()
            for k, a in arrays.items()]
    out = nc.dram_tensor("out_0", (N, H), F32, kind="ExternalOutput").ap()
    gnn_kernel(nc, *args, out)
    r = run_bass_kernel_spmd(nc, [{f"in_{k}": a for k, a in arrays.items()}], core_ids=[0])
    return r.results[0]["out_0"]
```

```python
import math
import concourse.bass as bass
from concourse import mybir
from contextlib import ExitStack

N, H, E, NT = 12500, 128, 200000, 9
P = 128
G = 4
TILES = 1564
T0 = 428
NG = TILES - T0
GROUPS = NG // G
EP = TILES * P
W = 96
D = 15
NB = 3
DB = D // NB
HI = 98
TAIL = N - (HI - 1) * P
BC = DB * HI
RING = 34
KB = 3
ROUNDS = TILES // RING
GP = 384
DP = 512
BN = 256
LOW0 = 3 * BN
CB0 = 5
DCAP = BN * CB0
R = 16 * BN
NBLK = (N + BN - 1) // BN
ACC = N + 100
DUMP = N
EPS = 1e-5
MARGIN = 130.0
PARTS = 4
XC = 7
XH = HI // XC
LEAD = 2
REST = 20
DW = DCAP + D + 1
XS = 3 * HI * H // 2

F32 = mybir.dt.float32
BF16 = mybir.dt.bfloat16
F16 = mybir.dt.float16
I32 = mybir.dt.int32
U16 = mybir.dt.uint16
ALU = mybir.AluOpType
ACT = mybir.ActivationFunctionType
AX = mybir.AxisListType.X
ET = mybir.EngineType


def place(rank):
    return N * (rank / E) ** 2


def dense_groups():
    out, t = [], 0
    while t < T0:
        best = 1
        for k in (2, 3, 4, 5, 6, 8, 12, 16):
            r = (t + k) * P
            per_node = E * E / (2.0 * N * r)
            if place(r) - place(t * P) + 5.5 * math.sqrt(P * k) / per_node + 1 <= D - 1:
                best = k
        best = min(best, T0 - t)
        out.append((t, best))
        t += best
    while len(out) % 4:
        i = max(range(len(out)), key=lambda j: out[j][1])
        t, k = out[i]
        out[i:i + 1] = [(t, k - k // 2), (t + k - k // 2, k // 2)]
    return out


DG = dense_groups()
QUADS = len(DG) // 4


def runs():
    out = []
    for j, (t, k) in enumerate(DG):
        if out and out[-1][2] == k:
            out[-1][3] += 1
        else:
            out.append([j, t, k, 1])
    return out


STAGES = ("hh", "ms", "ih", "rz", "t2", "th", "yt", "turn", "bn", "sd", "ln")
SLOTS = (("hh", "ms"), ("ih", "rz"), ("t2", "th", "zero"), ("yt",), ("turn",), ("bn", "sd"), ("ln",))


def dense_units():
    units = []
    for q in range(QUADS + 1):
        for s in range(4):
            if q < QUADS:
                t, k = DG[4 * q + s]
                units += [(0.75, ("B", 4 * q + s, e)) for e in range(t, t + k)]
            if q:
                units.append((2.2, ("F", q - 1, s)))
        if q:
            units.append((0.0, ("A", q - 1)))
    return units


def schedule():
    units = dense_units()
    total = sum(w for w, _ in units)
    items, lb, ub, low, clear = [], [], [], LOW0, LOW0 + R
    blocks = list(range(CB0, NBLK))
    done, spent, busy, late = 0, 0.0, [], False
    for g in range(GROUPS):
        lb.append(float(low))
        ub.append(float(clear - W))
        assert place(min(E, T0 * P + 512 * (g + 1))) + MARGIN < clear - W
        chunks = [[("G", g)]]
        if g < XC:
            chunks.append([("X", g)])
        while units and g >= LEAD and spent <= total * (g - LEAD) / (GROUPS - REST - LEAD):
            w, u = units.pop(0)
            spent += w
            chunks.append([u])
        if not units and not late and low > DCAP:
            late = True
            blocks = list(range(CB0)) + blocks
        for c in range(2):
            if not busy and blocks:
                b = blocks[0]
                if b < CB0 or place(min(E, T0 * P + 512 * (g + 1))) - MARGIN >= BN * (b + 1) or g == GROUPS - 1:
                    blocks.pop(0)
                    busy = [[(s, done, b) for s in slot if s != "zero" or b >= CB0] for slot in SLOTS]
                    if b >= CB0:
                        low = BN * (b + 1)
                        if b == CB0:
                            busy[0].insert(0, ("merge",))
                        elif (BN * b - LOW0) % R == 0:
                            busy[0].insert(0, ("wrap", b))
                    done += 1
            if busy:
                slot = busy.pop(0)
                for it in slot:
                    if it[0] == "zero":
                        clear = BN * (it[2] + 1) + R
                chunks[0 if c == 0 else (len(chunks) + 1) // 2 if len(chunks) > 1 else -1].extend(slot)
        for c in chunks:
            items += c
    assert not units and late
    for slot in busy:
        items += slot
    for b in blocks:
        items += [(s, done, b) for s in STAGES]
        done += 1
    return items, lb, ub


ITEMS, LB, UB = schedule()
ORDER = [it[2] for it in ITEMS if it[0] == "hh"]


def updates_before():
    n, out = 0, {}
    for it in ITEMS:
        out[it] = n
        n += {"G": 1, "A": 8, "zero": 1, "merge": 2, "wrap": 2}.get(it[0], 0)
    return out


BEFORE = updates_before()


def gnn_kernel(nc, x, xT, srcT, dstT, dstG, dstD, dstE, typT, low, wmT, bmsg, emb, wihT, whhT, bih, bhh, out):
    ctx = ExitStack()
    with ctx:
        def sb(name, shape, dt=F32):
            return ctx.enter_context(nc.sbuf_tensor(name, shape, dt))

        def pb(name, shape):
            return ctx.enter_context(nc.psum_tensor(name, shape, F32))

        def sem(name):
            return ctx.enter_context(nc.semaphore(name))

        mem = sb("mem", [P, XS + 2 * (R + W) + 2 * DW])
        xs = mem[:, 0:XS].bitcast(BF16).rearrange("p (c h f) -> p c h f", c=3, h=HI)
        ring = mem[:, XS:XS + 2 * (R + W)].rearrange("p (a n) -> p a n", a=2)
        den = mem[:, XS + 2 * (R + W):XS + 2 * (R + W) + 2 * DW].rearrange("p (a n) -> p a n", a=2)
        whole = mem[:, 0:2 * ACC].rearrange("p (a n) -> p a n", a=2)
        bbufs = sb("bbufs", [P, 2, HI * 4 * D], F16)
        Bb = [bbufs[:, k, :].rearrange("p (h d) -> p h d", h=HI) for k in range(2)]
        bbuf = bbufs[:, :, :].rearrange("p a n -> p (a n)").bitcast(F32)
        x1 = bbuf[:, HI * 2 * D:HI * 2 * D + XH * H].rearrange("p (h f) -> p h f", h=XH)
        gI = bbuf[:, 0:1536].bitcast(I32).rearrange("p (j e) -> p j e", j=3)
        dstI = bbuf[:, 1536:1536 + TILES].bitcast(I32)
        typI = bbuf[:, 3100:3100 + TILES].bitcast(I32)
        hiI = bbuf[:, 4664:4664 + T0].bitcast(I32)
        loI = bbuf[:, 5092:5092 + T0].bitcast(I32)
        idx = sb("idx", [P, TILES], I32)
        rel = sb("rel", [P, GROUPS, G], F16)
        key = sb("key", [P, T0], F16)
        lo = sb("lo", [P, T0], F16)
        dre = sb("dre", [P, T0], F16)
        typ = sb("typ", [P, TILES], F16)
        gbI = sb("gbI", [1, GROUPS], I32)
        dbI = sb("dbI", [1, len(DG)], I32)
        chk = bbuf[0:1, 5520:5520 + GROUPS]
        vi = sb("vi", [1, 8])
        flag = sb("flag", [1, 1], I32)
        dbase = sb("dbase", [P, len(DG)])
        dmax = sb("dmax", [1, len(DG)])
        iota = sb("iota", [P, D * HI], F16)
        iotaF = sb("iotaF", [P, W])
        ident = sb("ident", [P, P])
        xg = sb("xg", [P, RING, H])
        ohb = sb("ohb", [P, 2, G, W], BF16)
        ohf = sb("ohf", [P, 2, G, W])
        lbF = ohf[0:1, :, :, :].rearrange("p a g w -> p (a g w)")[:, 0:2 * GROUPS].rearrange("p (a g) -> p a g", a=2)
        tohb = sb("tohb", [P, 2, G, NT], BF16)
        ohk = sb("ohk", [P, KB, D * HI], BF16)
        ohl = sb("ohl", [P, KB, P], BF16)
        ohd = sb("ohd", [P, KB, D], BF16)
        tohd = sb("tohd", [P, KB, NT], BF16)
        tohs = sb("tohs", [P, NT])
        spare = sb("spare", [P, 1])
        mm = sb("mm", [P, 2, 3])
        md = sb("md", [P, 2, 4])
        cb = sb("cb", [NT, 2, 4 * D])
        wm = sb("wm", [P, H])
        em = sb("em", [NT, H])
        bmb = sb("bmb", [NT, H])
        wih = sb("wih", [P, 3 * H])
        whh = sb("whh", [P, 3 * H])
        bi = sb("bi", [P, 3])
        bh = sb("bh", [P, 3])
        bs = sb("bs", [P, 2])
        eps = sb("eps", [P, 1])
        xb = sb("xb", [P, 2, BN])
        arena = sb("arena", [P, 8 * BN])
        x2 = arena[:, 0:XH * H].rearrange("p (h f) -> p h f", h=XH)
        rz = arena[:, 0:2 * BN].rearrange("p (a n) -> p a n", a=2)
        tn = arena[:, 2 * BN:5 * BN].rearrange("p (a n) -> p a n", a=3)
        yT = arena[:, 5 * BN:6 * BN]
        msg = yT
        yo = arena[:, 6 * BN:8 * BN].rearrange("p (a s h) -> p a s h", a=2, s=2)
        gm = arena[:, 0:2 * GP].rearrange("p (a g) -> p a g", a=2)
        dm = arena[:, 768:768 + 2 * DP].rearrange("p (a g) -> p a g", a=2)
        dI = mem[:, 0:512].bitcast(I32).rearrange("p (j e) -> p j e", j=4)
        st = sb("st", [P, 2, 6])
        mv = sb("mv", [P, 2, 2])
        rs = sb("rs", [P, 2])
        sd = sb("sd", [P, 2])

        g_d = nc.dram_tensor("g_scratch", (2 * GP,), F32, kind="Internal").ap()
        d_d = nc.dram_tensor("d_scratch", (2 * DP,), F32, kind="Internal").ap()

        psb = pb("psb", [P, NB, 512])
        psf = pb("psf", [P, 512])
        psg = pb("psg", [P, 512])
        pA = pb("pA", [P, 512])
        pB = pb("pB", [P, 512])
        pC = pb("pC", [P, 512])
        g2 = psg[:, 0:2 * W].rearrange("p (a w) -> p a w", a=2)
        g2s = psg[:, 0:2 * P].rearrange("p (a w) -> p a w", a=2)

        names = ("s_idx s_gl s_dl s_dt s_tl s_lb s_w s_io s_id s_d s_mg s_md s_sg s_sd2 s_bg s_bd2 s_fl "
                 "s_used s_oh s_of s_grp s_acc s_ok  s_kd s_bd s_eb s_fd s_toh s_tr s_sl s_main "
                 "s_pm s_ms s_hh s_pg s_rz s_t2 s_n s_y s_pt s_mv s_sd s_ln s_xd s_xb s_xc s_xe s_xl").split()
        S = {n: sem(n) for n in names}
        s_g = [sem(f"s_g{i}") for i in range(RING)]
        s_x = [sem(f"s_x{i}") for i in range(2)]
        s_o = [sem(f"s_o{i}") for i in range(2)]

        def size(b):
            n = min(BN, N - b * BN)
            return b * BN, n, n // 2

        def read_flag(engine):
            return nc.values_load(flag[0:1, 0:1], engines=[engine], min_val=0, max_val=4 * GP,
                                  skip_runtime_bounds_check_because="a count of violated conditions")

        def store(sp, i):
            n0, n, q = size(ORDER[i])
            sp.wait_ge(S["s_ln"], i + 1)
            sp.dma_start(out[n0:n0 + n, :].rearrange("(p s) h -> p (s h)", s=2),
                         yo[0:q, i % 2, :, :].rearrange("p s h -> p (s h)")).then_inc(s_o[i % 2], 16)

        block = ctx.enter_context(nc.Block())

        @block.sync
        def _(sp):
            sp.dma_start(gI[:, :, :], dstG).then_inc(S["s_gl"], 16)
            sp.dma_start(dstI, dstT).then_inc(S["s_dt"], 16)
            sp.dma_start(typI, typT).then_inc(S["s_tl"], 16)
            sp.dma_start(lbF, low.rearrange("o (a g) -> o a g", a=2)).then_inc(S["s_lb"], 16)
            sp.wait_ge(S["s_mg"], 1)
            sp.dma_start(g_d.rearrange("(a p j) -> p a j", a=2, j=3), mm[:, :, :]).then_inc(S["s_sg"], 16)
            sp.wait_ge(S["s_sg"], 16)
            sp.dma_start(gm.rearrange("p a g -> p (a g)"), g_d.partition_broadcast(P)).then_inc(S["s_bg"], 16)
            sp.wait_ge(S["s_md"], 1)
            sp.dma_start(d_d.rearrange("(a p j) -> p a j", a=2, j=4), md[:, :, :]).then_inc(S["s_sd2"], 16)
            sp.wait_ge(S["s_sd2"], 16)
            sp.dma_start(dm.rearrange("p a g -> p (a g)"), d_d.partition_broadcast(P)).then_inc(S["s_bd2"], 16)
            sp.wait_ge(S["s_fl"], 1)
            bad = read_flag(ET.SP)
            with sp.If(bad == 0):
                for c in range(XC):
                    if c:
                        sp.wait_ge(S["s_xb"], c)
                    h0 = c * XH
                    h1 = min(h0 + XH, HI - 1)
                    sp.dma_start(x1[:, 0:h1 - h0, :],
                                 x[h0 * P:h1 * P, :].rearrange("(h p) f -> p h f", p=P)).then_inc(S["s_xd"], 16)
                sp.dma_start(x1[0:TAIL, XH - 1, :], x[(HI - 1) * P:N, :]).then_inc(S["s_xd"], 16)
            for i, b in enumerate(ORDER):
                n0, n, q = size(b)
                if i >= 2:
                    sp.wait_ge(S["s_y"], i - 1)
                sp.dma_start(xb[:, i % 2, 0:n], xT[:, n0:n0 + n]).then_inc(s_x[i % 2], 16)
                if i >= 2:
                    store(sp, i - 2)
            for i in range(NBLK - 2, NBLK):
                store(sp, i)
            for j in range(2):
                sp.wait_ge(s_o[j], 16 * len(ORDER[j::2]))

        @block.gpsimd
        def _(pool):
            pool.iota(iota[:, :], [[1, D * HI]], base=0, channel_multiplier=0,
                      allow_small_or_imprecise_dtypes=True).then_inc(S["s_io"], 1)
            pool.iota(iotaF[:, :], [[1, W]], base=0, channel_multiplier=0,
                      allow_small_or_imprecise_dtypes=True).then_inc(S["s_io"], 1)
            pool.memset(ident[:, :], 0.0).then_inc(S["s_id"], 1)
            pool.wait_ge(S["s_id"], 1)
            pool.affine_select(out=ident[:, :], in_=ident[:, :], compare_op=ALU.not_equal, fill=1.0,
                               base=0, pattern=[[-1, P]], channel_multiplier=1).then_inc(S["s_id"], 1)
            pool.wait_ge(S["s_idx"], 16)

            def gather(p):
                if p >= RING:
                    pool.wait_ge(S["s_used"], p - RING + 1)
                pool.indirect_dma_start(
                    out=xg[:, p % RING, :], out_offset=None, in_=x,
                    in_offset=bass.IndirectOffsetOnAxis(ap=idx[:, p:p + 1], axis=0),
                ).then_inc(s_g[p % RING], 16)

            for p in range(NG):
                gather(p)
            pool.wait_ge(S["s_fl"], 1)
            bad = read_flag(ET.Pool)
            with pool.If(bad > 0):
                for p in range(NG, TILES):
                    gather(p)

        @block.vector
        def _(v):
            cnt = [0]

            def link(ins):
                cnt[0] += 1
                ins.then_inc(S["s_d"], 1)
                v.wait_ge(S["s_d"], cnt[0])

            def more(ins):
                cnt[0] += 1
                ins.then_inc(S["s_d"], 1)

            def settle():
                v.wait_ge(S["s_d"], cnt[0])

            v.wait_ge(S["s_gl"], 16)
            v.tensor_reduce(mm[:, 0, :], gI, AX, ALU.min)
            v.tensor_reduce(mm[:, 1, :], gI, AX, ALU.max).then_inc(S["s_mg"], 1)
            v.wait_ge(S["s_dl"], 16)
            v.tensor_reduce(md[:, 0, :], dI, AX, ALU.min)
            v.tensor_reduce(md[:, 1, :], dI, AX, ALU.max).then_inc(S["s_md"], 1)
            more(v.memset(vi[:, :], 0.0))
            v.wait_ge(S["s_tl"], 16)
            more(v.tensor_copy(typ[:, :], typI))
            v.wait_ge(S["s_dt"], 16)
            v.wait_ge(S["s_bg"], 16)
            more(v.tensor_tensor(rel[:, :, :], dstI[:, 0:NG].rearrange("p (g t) -> p g t", t=G),
                                 gm[:, 0, 0:GROUPS].unsqueeze(2).to_broadcast([P, GROUPS, G]), ALU.subtract))
            v.memset(ring[:, :, :], 0.0)
            v.memset(den[:, :, :], 0.0)
            v.memset(psg[:, :], 0.0)
            more(v.memset(eps[:, :], EPS))

            settle()
            v.wait_ge(S["s_lb"], 16)
            g0 = gm[0:1, 0, 0:GROUPS]
            link(v.tensor_tensor(chk, gm[0:1, 1, 0:GROUPS], g0, ALU.subtract))
            link(v.tensor_scalar(chk, chk, float(W), None, ALU.is_ge))
            link(v.tensor_reduce(vi[:, 0:1], chk, AX, ALU.add))
            link(v.tensor_tensor(chk, lbF[:, 0, :], g0, ALU.is_gt))
            link(v.tensor_reduce(vi[:, 1:2], chk, AX, ALU.add))
            link(v.tensor_tensor(chk, lbF[:, 1, :], g0, ALU.is_lt))
            link(v.tensor_reduce(vi[:, 2:3], chk, AX, ALU.add))
            for _ in range(2):
                link(v.tensor_scalar(chk, g0, float(LOW0 + R), float(R), ALU.is_ge, ALU.mult))
                link(v.tensor_tensor(g0, g0, chk, ALU.subtract))
            more(v.tensor_scalar(gbI[:, :], g0, float(LOW0), None, ALU.subtract))

            v.wait_ge(S["s_bd2"], 16)
            v.wait_ge(S["s_idx"], 16)
            for j, t, k, n in runs():
                more(v.tensor_reduce(dbase[:, j:j + n],
                                     dm[:, 0, t:t + n * k].rearrange("p (n k) -> p n k", k=k), AX, ALU.min))
                more(v.tensor_reduce(dmax[:, j:j + n],
                                     dm[0:1, 1, t:t + n * k].rearrange("p (n k) -> p n k", k=k), AX, ALU.max))
            more(v.tensor_scalar(hiI, idx[:, NG:TILES], 7, None, ALU.arith_shift_right))
            more(v.tensor_scalar(loI, idx[:, NG:TILES], P - 1, None, ALU.bitwise_and))
            settle()
            more(v.tensor_copy(lo[:, :], loI))
            more(v.tensor_copy(dbI[:, :], dbase[0:1, :]))
            for j, t, k, n in runs():
                more(v.tensor_tensor(dre[:, t:t + n * k].rearrange("p (n k) -> p n k", k=k),
                                     dstI[:, NG + t:NG + t + n * k].rearrange("p (n k) -> p n k", k=k),
                                     dbase[:, j:j + n].unsqueeze(2).to_broadcast([P, n, k]), ALU.subtract))
            settle()
            more(v.scalar_tensor_tensor(out=key[:, :], in0=dre[:, :], scalar=float(HI), in1=hiI,
                                        op0=ALU.mult, op1=ALU.add))
            nd = len(DG)
            link(v.tensor_scalar(chk[:, 0:nd], dmax[:, :], float(DCAP), None, ALU.is_ge))
            link(v.tensor_reduce(vi[:, 3:4], chk[:, 0:nd], AX, ALU.add))
            link(v.tensor_tensor(chk[:, 0:nd], dmax[:, :], dbase[0:1, :], ALU.subtract))
            link(v.tensor_scalar(chk[:, 0:nd], chk[:, 0:nd], float(D), None, ALU.is_ge))
            link(v.tensor_reduce(vi[:, 4:5], chk[:, 0:nd], AX, ALU.add))
            link(v.tensor_reduce(chk[:, 0:1], vi[:, :], AX, ALU.add))
            v.tensor_copy(flag[:, :], chk[:, 0:1]).then_inc(S["s_fl"], 1)
            v.wait_ge(S["s_w"], 16 * 7)
            more(v.tensor_tensor(em[:, :], em[:, :], bmb[:, :], ALU.add))
            link(v.tensor_tensor(bs[:, :], bi[:, 0:2], bh[:, 0:2], ALU.add))
            v.wait_ge(S["s_io"], 2)
            v.wait_ge(S["s_fl"], 1)
            bad = read_flag(ET.DVE)

            def final(kind, i, b, slow, seen):
                n0, n, q = size(b)
                r = rz[:, :, 0:n]
                o = (n0 - LOW0) % R
                t = tn[:, :, 0:n]
                xx = xb[:, i % 2, 0:n]
                if kind == "t2":
                    v.wait_ge(S["s_rz"], 2 * i + 2)
                    v.wait_ge(S["s_pg"], i + 1)
                    link(v.scalar_tensor_tensor(out=t[:, 0, :], in0=pB[:, 0:n], scalar=bh[:, 2:3],
                                                in1=r[:, 0, :], op0=ALU.add, op1=ALU.mult))
                    v.tensor_tensor(t[:, 1, :], t[:, 0, :], pB[:, BN:BN + n], ALU.add).then_inc(S["s_t2"], 1)
                elif kind == "yt":
                    v.wait_ge(S["s_n"], i + 1)
                    more(v.tensor_tensor(t[:, 0, :], xx, t[:, 2, :], ALU.subtract))
                    more(v.tensor_tensor(t[:, 1, :], xx, t[:, 2, :], ALU.add))
                    v.wait_ge(S["s_d"], cnt[0] - 1)
                    link(v.tensor_tensor(t[:, 0, :], t[:, 0, :], r[:, 1, :], ALU.mult))
                    v.wait_ge(S["s_pg"], i + 1)
                    v.tensor_tensor(yT[:, 0:n], t[:, 0, :], t[:, 1, :], ALU.add).then_inc(S["s_y"], 1)
                elif kind == "bn":
                    v.wait_ge(S["s_pt"], i + 1)
                    for s in range(2):
                        more(v.bn_stats(st[0:q, s, :], pC[0:q, BN + s * H:BN + (s + 1) * H]))
                    for s in range(2):
                        v.wait_ge(S["s_d"], cnt[0] - 1 + s)
                        ins = v.bn_aggr(mv[0:q, s, :], st[0:q, s, :])
                    ins.then_inc(S["s_mv"], 1)
                elif kind == "ln":
                    v.wait_ge(S["s_sd"], i + 1)
                    if i >= 2:
                        v.wait_ge(s_o[i % 2], 16 * (i // 2))
                    link(v.reciprocal(rs[0:q, :], sd[0:q, :]))
                    for s in range(2):
                        ins = v.tensor_scalar(yo[0:q, i % 2, s, :], pC[0:q, BN + s * H:BN + (s + 1) * H],
                                              mv[0:q, s, 0:1], rs[0:q, s:s + 1], ALU.subtract, ALU.mult)
                    ins.then_inc(S["s_ln"], 1)
                    v.wait_ge(S["s_ln"], i + 1)

                elif kind == "zero":
                    v.wait_ge(S["s_pm"], i + 1)
                    v.wait_ge(S["s_acc"], seen)
                    v.memset(ring[:, :, o:o + n], 0.0).then_inc(S["s_acc"], 1)

            linked = cnt[0]
            with v.If(bad == 0):
                settle()
                regs = {}

                def prepare(it):
                    if it[0] == "G":
                        g = it[1]
                        b = g % 2
                        if g >= 2:
                            v.wait_ge(S["s_grp"], g - 1)
                        v.tensor_tensor(ohb[:, b, :, :], rel[:, g, :].unsqueeze(2).to_broadcast([P, G, W]),
                                        iotaF[:, :].unsqueeze(1).to_broadcast([P, G, W]), ALU.is_equal)
                        v.tensor_tensor(tohb[:, b, :, :],
                                        typ[:, g * G:g * G + G].unsqueeze(2).to_broadcast([P, G, NT]),
                                        iotaF[:, 0:NT].unsqueeze(1).to_broadcast([P, G, NT]),
                                        ALU.is_equal).then_inc(S["s_oh"], 1)
                    elif it[0] == "B":
                        _, j, e = it
                        b = e % KB
                        if e >= KB:
                            v.wait_ge(S["s_kd"], e - KB + 1)
                        v.tensor_scalar(ohd[:, b, :], iota[:, 0:D], dre[:, e:e + 1], None, ALU.is_equal)
                        v.tensor_scalar(tohd[:, b, :], iota[:, 0:NT], typ[:, NG + e:NG + e + 1], None,
                                        ALU.is_equal)
                        v.tensor_scalar(ohl[:, b, :], iota[:, 0:P], lo[:, e:e + 1], None, ALU.is_equal)
                        v.tensor_scalar(ohk[:, b, :], iota[:, :], key[:, e:e + 1], None,
                                        ALU.is_equal).then_inc(S["s_ok"], 1)

                def load_bases(table, at, k, hi):
                    _, vals = nc.values_load_multi_w_load_instructions(
                        table[0:1, at:at + k], engines=[ET.DVE], min_val=0, max_val=hi,
                        skip_runtime_bounds_check_because="the least destination of a group is a node")
                    return vals

                def consume(it):
                    seen = BEFORE[it]
                    if it[0] == "G":
                        g = it[1]
                        if g % 4 == 0:
                            for j, q in enumerate(load_bases(gbI, g, min(4, GROUPS - g), R - 1)):
                                regs[g + j] = q
                        v.wait_ge(S["s_grp"], g + 1)
                        if seen:
                            v.wait_ge(S["s_acc"], seen)
                        d = ring[:, :, bass.ds(regs[g], W)]
                        v.tensor_tensor(d, d, g2[:, :, :], ALU.add).then_inc(S["s_acc"], 1)
                    elif it[0] == "X":
                        c = it[1]
                        v.wait_ge(S["s_xc"], c + 1)
                        v.tensor_tensor(x2, x1, xs[:, 0, c * XH:(c + 1) * XH, :],
                                        ALU.subtract).then_inc(S["s_xb"], 1)
                        v.wait_ge(S["s_xe"], c + 1)
                        v.tensor_tensor(xs[:, 2, c * XH:(c + 1) * XH, :], x2, xs[:, 1, c * XH:(c + 1) * XH, :],
                                        ALU.subtract).then_inc(S["s_xl"], 1)
                        v.wait_ge(S["s_xl"], c + 1)
                    elif it[0] == "merge":
                        v.wait_ge(S["s_acc"], seen)
                        m = den[:, :, LOW0:DCAP]
                        v.tensor_tensor(m, m, ring[:, :, 0:DCAP - LOW0], ALU.add).then_inc(S["s_acc"], 1)
                        v.wait_ge(S["s_acc"], seen + 1)
                        v.memset(ring[:, :, 0:DCAP - LOW0], 0.0).then_inc(S["s_acc"], 1)
                    elif it[0] == "wrap":
                        v.wait_ge(S["s_acc"], seen)
                        m = ring[:, :, 0:W]
                        v.tensor_tensor(m, m, ring[:, :, R:R + W], ALU.add).then_inc(S["s_acc"], 1)
                        v.wait_ge(S["s_acc"], seen + 1)
                        v.memset(ring[:, :, R:R + W], 0.0).then_inc(S["s_acc"], 1)
                    elif it[0] == "A":
                        q = it[1]
                        bases = load_bases(dbI, 4 * q, 4, DCAP - 1)
                        v.wait_ge(S["s_fd"], q + 1)
                        for s in range(4):
                            v.wait_ge(S["s_acc"], seen + max(0, 2 * s - 1))
                            d = den[:, 0, bass.ds(bases[s], D)]
                            v.tensor_tensor(d, d, psf[:, s * D:(s + 1) * D], ALU.add).then_inc(S["s_acc"], 1)
                            if s:
                                v.wait_ge(S["s_acc"], seen + 2 * s)
                            c = den[0:NT, 1, bass.ds(bases[s], D)]
                            v.tensor_tensor(c, c, cb[:, q % 2, s * D:(s + 1) * D], ALU.add).then_inc(S["s_acc"], 1)
                    elif it[0] in STAGES or it[0] == "zero":
                        final(*it, False, seen)

                ahead = {None: [("G", 0)]}
                for kind, back in (("G", 1), ("B", KB - 1)):
                    own = [it for it in ITEMS if it[0] == kind]
                    for a, it in enumerate(own):
                        if it != ("G", 0):
                            ahead.setdefault(own[a - back] if a >= back else ("G", 0), []).append(it)
                for it in ahead[None]:
                    prepare(it)
                for it in ITEMS:
                    consume(it)
                    for nxt in ahead.get(it, []):
                        prepare(nxt)
            with v.Else():
                cnt[0] = linked
                settle()
                link(v.memset(mem[:, 0:2 * ACC], 0.0))
                with v.Fori(0, ROUNDS) as i:
                    for s in range(RING):
                        t = i * RING + s
                        v.wait_ge(S["s_tr"], t)
                        v.tensor_tensor(tohs[:, :], typ[:, bass.ds(t, 1)].to_broadcast([P, NT]),
                                        iotaF[:, 0:NT], ALU.is_equal).then_inc(S["s_toh"], 1)
                        v.wait_ge(S["s_tr"], t + 1)
                        v.memset(spare[:, :], 0.0)
                        with v.Fori(0, P) as e:
                            d = nc.values_load(dstE[0:1, bass.ds(t * P + e, 1)], engines=[ET.DVE],
                                               min_val=0, max_val=DUMP,
                                               skip_runtime_bounds_check_because="a destination is a node")
                            q = whole[:, :, bass.ds(d, 1)]
                            v.tensor_tensor(q, q, g2s[:, :, bass.ds(e, 1)], ALU.add)
                            v.drain()
                        v.drain().then_inc(S["s_sl"], 1)
                v.drain().then_inc(S["s_main"], 1)
                for i, b in enumerate(ORDER):
                    for s in STAGES:
                        final(s, i, b, True, 0)

        @block.tensor
        def _(pe):
            pe.wait_ge(S["s_fl"], 1)
            bad = read_flag(ET.PE)

            def final(kind, i, b, slow, seen):
                n0, n, q = size(b)
                xx = xb[:, i % 2, 0:n]
                if kind == "hh":
                    if slow:
                        pe.wait_ge(S["s_main"], 1)
                    else:
                        pe.wait_ge(S["s_acc"], seen)
                    o = (n0 - LOW0) % R
                    sums = whole[:, :, n0:n0 + n] if slow else \
                        den[:, :, n0:n0 + n] if b < CB0 else ring[:, :, o:o + n]
                    if i:
                        pe.wait_ge(S["s_ln"], i)
                    pe.matmul(pC[:, 0:n], wm[:, :], sums[:, 0, :], start=True, stop=False,
                              skip_group_check=True)
                    pe.matmul(pC[:, 0:n], em[:, :], sums[0:NT, 1, :], start=False, stop=True,
                              skip_group_check=True).then_inc(S["s_pm"], 1)
                    pe.wait_ge(s_x[i % 2], 16 * (i // 2 + 1))
                    if i:
                        pe.wait_ge(S["s_rz"], 2 * i)
                        pe.wait_ge(S["s_t2"], i)
                    for k, (bank, o) in enumerate(((pA, 0), (pA, BN), (pB, 0))):
                        pe.matmul(bank[:, o:o + n], whh[:, k * H:(k + 1) * H], xx, start=(o == 0),
                                  stop=(k == 2), skip_group_check=True)
                elif kind == "ih":
                    pe.wait_ge(S["s_ms"], i + 1)
                    for k, (bank, o) in enumerate(((pA, 0), (pA, BN), (pB, BN))):
                        ins = pe.matmul(bank[:, o:o + n], wih[:, k * H:(k + 1) * H], msg[:, 0:n], start=False,
                                        stop=True, skip_group_check=True)
                    ins.then_inc(S["s_pg"], 1)
                elif kind == "turn":
                    pe.wait_ge(S["s_y"], i + 1)
                    yv = yT[:, 0:n].rearrange("f (p s) -> f s p", s=2)
                    for s in range(2):
                        ins = pe.transpose(pC[0:q, BN + s * H:BN + (s + 1) * H], yv[:, s, :], ident[:, :])
                    ins.then_inc(S["s_pt"], 1)

            with pe.If(bad == 0):
                pe.wait_ge(S["s_id"], 2)
                for it in ITEMS:
                    if it[0] == "G":
                        g = it[1]
                        b = g % 2
                        pe.wait_ge(S["s_oh"], g + 1)
                        pe.wait_ge(S["s_of"], g + 1)
                        if g:
                            pe.wait_ge(S["s_acc"], BEFORE[("G", g - 1)] + 1)
                        for j in range(G):
                            p = g * G + j
                            pe.wait_ge(s_g[p % RING], 16 * (p // RING + 1))
                            pe.matmul(g2[:, 0, :], xg[:, p % RING, :], ohf[:, b, j, :], start=(j == 0),
                                      stop=(j == G - 1), skip_group_check=True).then_inc(S["s_used"], 1)
                        for j in range(G):
                            ins = pe.matmul(g2[0:NT, 1, :], tohb[:, b, j, :], ohb[:, b, j, :], start=False,
                                            stop=(j == G - 1), skip_group_check=True)
                        ins.then_inc(S["s_grp"], 1)
                    elif it[0] == "B":
                        _, j, e = it
                        t_j, k_j = DG[j]
                        first, last = e == t_j, e == t_j + k_j - 1
                        pe.wait_ge(S["s_ok"], e + 1)
                        b = e % KB
                        for i in range(NB):
                            if j and first:
                                pe.wait_ge(S["s_eb"], 3 * (j - 1) + i + 1)
                            pe.matmul(psb[:, i, 0:BC], ohl[:, b, :], ohk[:, b, i * BC:(i + 1) * BC],
                                      start=first, stop=last, skip_group_check=True)
                        pe.matmul(psb[0:NT, 0, BC:BC + D], tohd[:, b, :], ohd[:, b, :], start=False,
                                  stop=last, skip_group_check=True).then_inc(S["s_kd"], 1)
                    elif it[0] == "F":
                        _, q, f = it
                        if f == 0:
                            pe.wait_ge(S["s_eb"], 3 * (4 * q + 4))
                            if q == 0:
                                pe.wait_ge(S["s_xl"], XC)
                            else:
                                pe.wait_ge(S["s_acc"], BEFORE[("A", q - 1)] + 8)
                        for h in range(HI * f // PARTS, HI * (f + 1) // PARTS):
                            kk = P if h < HI - 1 else TAIL
                            for c in range(3):
                                ins = pe.matmul(psf[:, 0:4 * D], xs[0:kk, c, h, :], Bb[q % 2][0:kk, h, :],
                                                start=(h == 0 and c == 0), stop=(h == HI - 1 and c == 2),
                                                skip_group_check=True)
                        if f == PARTS - 1:
                            ins.then_inc(S["s_fd"], 1)
                    elif it[0] in STAGES:
                        final(*it, False, BEFORE[it])
            with pe.Else():
                pe.wait_ge(S["s_id"], 2)
                with pe.Fori(0, ROUNDS) as i:
                    for s in range(RING):
                        t = i * RING + s
                        pe.wait_ge(s_g[s], (i + 1) * 16)
                        pe.wait_ge(S["s_toh"], t + 1)
                        pe.wait_ge(S["s_sl"], t)
                        pe.transpose(g2s[:, 0, :], xg[:, s, :], ident[:, :]).then_inc(S["s_used"], 1)
                        pe.transpose(g2s[0:NT, 1, :], tohs[:, :], ident[:, :]).then_inc(S["s_tr"], 1)
                for i, b in enumerate(ORDER):
                    for s in STAGES:
                        final(s, i, b, True, 0)

        @block.scalar
        def _(act):
            act.dma_start(idx[:, :], srcT).then_inc(S["s_idx"], 16)
            act.dma_start(dI, dstD).then_inc(S["s_dl"], 16)
            act.dma_start(wm[:, :], wmT).then_inc(S["s_w"], 16)
            act.dma_start(em[:, :], emb).then_inc(S["s_w"], 16)
            act.dma_start(bmb[:, :], bmsg.partition_broadcast(NT)).then_inc(S["s_w"], 16)
            act.dma_start(wih[:, :], wihT).then_inc(S["s_w"], 16)
            act.dma_start(whh[:, :], whhT).then_inc(S["s_w"], 16)
            act.dma_start(bi[:, :], bih).then_inc(S["s_w"], 16)
            act.dma_start(bh[:, :], bhh).then_inc(S["s_w"], 16)
            act.wait_ge(S["s_fl"], 1)
            bad = read_flag(ET.Activation)

            def final(kind, i, b):
                n0, n, q = size(b)
                if kind == "ms":
                    act.wait_ge(S["s_pm"], i + 1)
                    if i:
                        act.wait_ge(S["s_pt"], i)
                    act.copy(msg[:, 0:n], pC[:, 0:n]).then_inc(S["s_ms"], 1)
                elif kind == "rz":
                    act.wait_ge(S["s_pg"], i + 1)
                    if i:
                        act.wait_ge(S["s_y"], i)
                    for k in range(2):
                        act.activation(rz[:, k, 0:n], pA[:, k * BN:k * BN + n], ACT.Sigmoid,
                                       bias=bs[:, k:k + 1]).then_inc(S["s_rz"], 1)
                elif kind == "th":
                    act.wait_ge(S["s_t2"], i + 1)
                    act.activation(tn[:, 2, 0:n], tn[:, 1, 0:n], ACT.Tanh, bias=bi[:, 2:3]).then_inc(S["s_n"], 1)
                elif kind == "sd":
                    act.wait_ge(S["s_mv"], i + 1)
                    if i:
                        act.wait_ge(S["s_ln"], i)
                    act.activation(sd[0:q, :], mv[0:q, :, 1], ACT.Sqrt, bias=eps[0:q, 0:1]).then_inc(S["s_sd"], 1)

            with act.If(bad == 0):
                def widen(g):
                    act.wait_ge(S["s_oh"], g + 1)
                    if g >= 2:
                        act.wait_ge(S["s_grp"], g - 1)
                    act.copy(ohf[:, g % 2, :, :], ohb[:, g % 2, :, :]).then_inc(S["s_of"], 1)

                widen(0)
                for it in ITEMS:
                    if it[0] == "G":
                        if it[1] + 1 < GROUPS:
                            widen(it[1] + 1)
                    elif it[0] == "X":
                        c = it[1]
                        act.wait_ge(S["s_xd"], 16 * (c + 1) + (16 if c == XC - 1 else 0))
                        act.copy(xs[:, 0, c * XH:(c + 1) * XH, :], x1).then_inc(S["s_xc"], 1)
                        act.wait_ge(S["s_xb"], c + 1)
                        act.copy(xs[:, 1, c * XH:(c + 1) * XH, :], x2).then_inc(S["s_xe"], 1)
                    elif it[0] == "B":
                        _, j, e = it
                        if e == sum(DG[j]) - 1:
                            q, s = j // 4, j % 4
                            act.wait_ge(S["s_kd"], e + 1)
                            if s == 0 and q >= 2:
                                act.wait_ge(S["s_fd"], q - 1)
                                act.wait_ge(S["s_acc"], BEFORE[("A", q - 2)] + 8)
                            if j == 4:
                                act.wait_ge(S["s_xb"], XC)
                            for i in range(NB):
                                o = s * D + i * DB
                                ins = act.copy(Bb[q % 2][:, :, o:o + DB].rearrange("p h d -> p d h"),
                                               psb[:, i, 0:BC].rearrange("p (d h) -> p d h", d=DB))
                                if i == 0:
                                    ins = act.copy(cb[:, q % 2, s * D:(s + 1) * D], psb[0:NT, 0, BC:BC + D])
                                ins.then_inc(S["s_eb"], 1)
                    elif it[0] in STAGES:
                        final(*it)
            with act.Else():
                for i, b in enumerate(ORDER):
                    for s in STAGES:
                        final(s, i, b)


def kernel(x, src, dst, edge_type_9, L0_gnn_W_msg, L0_gnn_b_msg, L0_gnn_edge_embed, L0_gnn_W_ih,
           L0_gnn_W_hh, L0_gnn_b_ih, L0_gnn_b_hh):
    import numpy as np
    import concourse.bacc as bacc
    from concourse.bass_utils import run_bass_kernel_spmd

    cut = T0 * P

    def lay(a):
        return np.ascontiguousarray(a)

    def turned(a, fill):
        a = np.asarray(a)
        return np.concatenate([a[cut:], np.full(EP - E, fill, a.dtype), a[:cut]])

    def by_tile(a, fill):
        return lay(turned(a, fill).reshape(TILES, P).T)

    def repeated(a, n):
        return np.concatenate([a, np.repeat(a[-1:], n - a.shape[0])])

    x, dst = np.asarray(x), np.asarray(dst)
    arrays = {
        "x": lay(x),
        "xT": lay(x.T),
        "srcT": by_tile(src, 0),
        "dstT": by_tile(dst, -1),
        "dstG": repeated(dst[cut:], GP * G * P).reshape(P, 3, G * P),
        "dstD": repeated(dst[:cut], DP * P).reshape(P, 4, P),
        "dstE": turned(dst, DUMP).reshape(1, EP),
        "typT": by_tile(edge_type_9, 0),
        "low": np.array([LB + UB], np.float32),
        "wmT": lay(np.asarray(L0_gnn_W_msg).T),
        "bmsg": lay(np.asarray(L0_gnn_b_msg)),
        "emb": lay(np.asarray(L0_gnn_edge_embed)),
        "wihT": lay(np.asarray(L0_gnn_W_ih).T),
        "whhT": lay(np.asarray(L0_gnn_W_hh).T),
        "bih": lay(np.asarray(L0_gnn_b_ih).reshape(3, H).T),
        "bhh": lay(np.asarray(L0_gnn_b_hh).reshape(3, H).T),
    }
    nc = bacc.Bacc("TRN2", target_bir_lowering=False, num_devices=1)
    args = [nc.dram_tensor(f"in_{k}", a.shape, mybir.dt.from_np(a.dtype), kind="ExternalInput").ap()
            for k, a in arrays.items()]
    out = nc.dram_tensor("out_0", (N, H), F32, kind="ExternalOutput").ap()
    gnn_kernel(nc, *args, out)
    r = run_bass_kernel_spmd(nc, [{f"in_{k}": a for k, a in arrays.items()}], core_ids=[0])
    return r.results[0]["out_0"]
```

```python
import math
import concourse.bass as bass
from concourse import mybir
from contextlib import ExitStack

N, H, E, NT = 12500, 128, 200000, 9
P = 128
G = 4
TILES = 1564
T0 = 492
NG = TILES - T0
GROUPS = NG // G
EP = TILES * P
W = 96
D = 15
NB = 3
DB = D // NB
HI = 98
TAIL = N - (HI - 1) * P
BC = DB * HI
RING = 23
KB = 4
ROUNDS = TILES // RING
GP = 384
DP = 512
BN = 256
LOW0 = 4 * BN
CB0 = 6
DCAP = BN * CB0
R = 13 * BN
NBLK = (N + BN - 1) // BN
ACC = N + 100
DUMP = N
EPS = 1e-5
MARGIN = 100.0
PARTS = 4
XU = 4
UNITS = -(-HI // XU)
PRE = 7
PER = 2
Z0 = 3
SETTLED = 8
LEAD = 5
REST = 4
AHEAD = 3
SWITCH = 22
STEPS = (2, 3)
SHIFT = 3
DW = DCAP + D + 1
XS = 3 * HI * H // 2

F32 = mybir.dt.float32
BF16 = mybir.dt.bfloat16
F16 = mybir.dt.float16
I32 = mybir.dt.int32
U16 = mybir.dt.uint16
ALU = mybir.AluOpType
ACT = mybir.ActivationFunctionType
AX = mybir.AxisListType.X
ET = mybir.EngineType


def place(rank):
    return N * (rank / E) ** 2


def width(g):
    r = min(E, T0 * P + 512 * (g + 1))
    nodes = 512 * 2.0 * N * r / (E * E)
    return min(W, 4 * math.ceil((nodes + 7.0 * math.sqrt(512.0) * nodes / 512 + 4) / 4))


def dense_groups():
    out, t = [], 0
    while t < T0:
        best = 1
        for k in (2, 3, 4, 5, 6, 8, 12, 16):
            r = (t + k) * P
            per_node = E * E / (2.0 * N * r)
            if place(r) - place(t * P) + 5.5 * math.sqrt(P * k) / per_node + 1 <= D - 1:
                best = k
        best = min(best, T0 - t)
        out.append((t, best))
        t += best
    while len(out) % 4:
        i = max(range(len(out)), key=lambda j: out[j][1])
        t, k = out[i]
        out[i:i + 1] = [(t, k - k // 2), (t + k - k // 2, k // 2)]
    return out


DG = dense_groups()
QUADS = len(DG) // 4


def runs():
    out = []
    for j, (t, k) in enumerate(DG):
        if out and out[-1][2] == k:
            out[-1][3] += 1
        else:
            out.append([j, t, k, 1])
    return out


STAGES = ("hh", "ms", "ih", "rz", "t2", "th", "yt", "turn", "bn", "sd", "ln")
SLOTS = (("hh", "ms"), ("ih", "rz"), (), ("t2", "th", "zero"), ("yt",), (), ("turn",), ("bn", "sd"), ("ln",))


def dense_units():
    units = []
    for q in range(QUADS + 1):
        for s in range(4):
            if q < QUADS:
                t, k = DG[4 * q + s]
                units += [(0.63, ("B", 4 * q + s, e)) for e in range(t, t + k)]
            if q:
                units.append((1.84, ("F", q - 1, s)))
        if q:
            units.append((0.0, ("A", q - 1)))
    return units


def schedule():
    units = dense_units()
    cost = {"hh": 3.1, "ih": 1.4, "turn": 0.3}
    total = sum(w for w, _ in units) + 4.8 * (NBLK - REST // 3) + 0.5 * (GROUPS - REST - LEAD)
    items, lb, ub, lbd, low, clear, lowd = [], [], [], [], LOW0, LOW0 + Z0 * BN, 0
    first, second, main = list(range(LOW0 // BN)), list(range(LOW0 // BN, CB0)), list(range(CB0, NBLK))
    done, spent, active, late, added = 0, 0.0, [], None, 0

    def pick(g, top):
        if first and (added == QUADS or place(DG[4 * added][0] * P) - MARGIN >= BN * (first[0] + 1)):
            return first.pop(0)
        if late is not None and second:
            return second.pop(0)
        if main and (g >= GROUPS or top - MARGIN >= BN * (main[0] + 1)):
            return main.pop(0)
        return None

    def step(g, top):
        nonlocal done, low, lowd, clear
        out = []
        for a in list(active):
            slot = a.pop(0)
            for it in slot:
                if it[0] == "zero":
                    clear = max(clear, BN * (it[2] + 1) + R)
            out += slot
            if not a:
                active.remove(a)
        if late is None:
            free = not active
        else:
            free = len(active) < 2 and (not active or len(SLOTS) - len(active[-1]) >= SHIFT - 1)
        b = pick(g, top) if free else None
        if b is not None:
            slots = [[(s, done, b) for s in slot if s != "zero" or b >= CB0] for slot in SLOTS]
            if b >= CB0:
                low = BN * (b + 1)
                if b == CB0:
                    slots[0].insert(0, ("merge",))
                elif (BN * b - LOW0) % R == 0:
                    slots[0].insert(0, ("wrap", b))
            elif b < LOW0 // BN:
                lowd = BN * (b + 1)
            done += 1
            active.append(slots)
        return out

    x = PRE
    for g in range(GROUPS):
        ub.append(float(clear - W))
        top = place(min(E, T0 * P + 512 * (g + 1)))
        assert top + MARGIN < clear - W
        chunks = [[("G", g)]]
        if g == 1:
            chunks.append([("dense",)])
        for _ in range(PER):
            if x < UNITS + 2:
                chunks.append([("X", x)])
                x += 1
        if Z0 <= g - SETTLED + Z0 < R // BN:
            chunks.append([("clear", g - SETTLED + Z0)])
            clear = LOW0 + BN * (g - SETTLED + Z0 + 1)
        if not units and late is None and low > DCAP:
            late = done
        n = STEPS[late is not None]
        outs = [step(g, place(T0 * P + 512 * g)) for _ in range(n)]
        lb.append(float(low))
        spent += sum(cost.get(it[0], 0.0) for out in outs for it in out) + (0.5 if g >= LEAD else 0.0)
        while units and g >= LEAD and spent <= total * (g - LEAD) / (GROUPS - REST - LEAD):
            w, u = units.pop(0)
            spent += w
            chunks.append([u])
            if u[0] == "A":
                lbd += 4 * [float(lowd)]
                added += 1
        chunks[min(1, len(chunks) - 1)].append(("GA", g))
        for c in range(n):
            chunks[max(min(1, len(chunks) - 1), (len(chunks) * c) // n)].extend(outs[c])
        for c in chunks:
            items += c
    assert not units and late is not None and x == UNITS + 2
    items.append(("end",))
    while active or first or second or main:
        items += step(GROUPS, N)
    return items, lb, ub, late, lbd


ITEMS, LB, UB, LATE, LBD = schedule()
WG = [width(g) for g in range(GROUPS)]
ORDER = [it[2] for it in ITEMS if it[0] == "hh"]


def updates_before():
    n, start, out = 0, 0, {}
    for it in ITEMS:
        if it[0] in ("G", "end"):
            start = n
        if it[0] == "hh":
            out[("sums", it[1])] = start
        out[it] = n
        if it[0] in ("merge", "wrap"):
            start = n + 2
        n += {"GA": 1, "A": 8, "zero": 1, "clear": 1, "merge": 2, "wrap": 2}.get(it[0], 0)
    return out


BEFORE = updates_before()


def wing(i, slow):
    return 0 if slow or i < LATE else (i - LATE + 1) % 2


def before(i, slow):
    j = i - 1
    while j >= 0 and wing(j, slow) != wing(i, slow):
        j -= 1
    return j + 1


def gnn_kernel(nc, x, xT, srcT, dstT, dstG, dstD, dstE, typT, low, wmT, bmsg, emb, wihT, whhT, bih, bhh, out):
    ctx = ExitStack()
    with ctx:
        def sb(name, shape, dt=F32):
            return ctx.enter_context(nc.sbuf_tensor(name, shape, dt))

        def pb(name, shape):
            return ctx.enter_context(nc.psum_tensor(name, shape, F32))

        def sem(name):
            return ctx.enter_context(nc.semaphore(name))

        mem = sb("mem", [P, XS + 2 * (R + W) + 2 * DW])
        xs = mem[:, 0:XS].bitcast(BF16).rearrange("p (h c f) -> p h c f", c=3, h=HI)
        ring = mem[:, XS:XS + 2 * (R + W)].rearrange("p (a n) -> p a n", a=2)
        den = mem[:, XS + 2 * (R + W):XS + 2 * (R + W) + 2 * DW].rearrange("p (a n) -> p a n", a=2)
        whole = mem[:, 0:2 * ACC].rearrange("p (a n) -> p a n", a=2)
        bbufs = sb("bbufs", [P, 2, HI * 4 * D], F16)
        Bb = [bbufs[:, k, :].rearrange("p (h d) -> p h d", h=HI) for k in range(2)]
        bbuf = bbufs[:, :, :].rearrange("p a n -> p (a n)").bitcast(F32)
        x1 = ring[:, 0, R - 4 * XU * H:R].rearrange("p (c n) -> p c n", c=4)
        gI = bbuf[:, 0:1536].bitcast(I32).rearrange("p (j e) -> p j e", j=3)
        dstI = bbuf[:, 1536:1536 + TILES].bitcast(I32)
        typI = bbuf[:, 3100:3100 + TILES].bitcast(I32)
        hiI = bbuf[:, 4664:4664 + T0].bitcast(I32)
        loI = bbuf[:, 4664 + T0:4664 + 2 * T0].bitcast(I32)
        idx = sb("idx", [P, TILES], I32)
        rel = sb("rel", [P, GROUPS, G], F16)
        key = sb("key", [P, T0], F16)
        lo = sb("lo", [P, T0], F16)
        dre = sb("dre", [P, T0], F16)
        typ = sb("typ", [P, TILES], F16)
        gbI = sb("gbI", [1, GROUPS], I32)
        dbI = sb("dbI", [1, len(DG)], I32)
        chk = bbuf[0:1, 0:3 * GROUPS + 3 * len(DG)]
        vi = sb("vi", [1, 8])
        flag = sb("flag", [1, 1], I32)
        dbase = sb("dbase", [P, len(DG)])
        dmax = sb("dmax", [1, len(DG)])
        iota = sb("iota", [P, D * HI], F16)
        iotaF = sb("iotaF", [P, W])
        ident = sb("ident", [P, P])
        nid = sb("nid", [P, P], BF16)
        xg = sb("xg", [P, RING, 3 * H], BF16)
        ohs = sb("ohs", [P, AHEAD, G * W])
        lbF = ohs[0:1, :, :].rearrange("p a w -> p (a w)")[:, 0:3 * GROUPS + len(DG)]
        tohb = sb("tohb", [P, AHEAD, G, NT], BF16)
        ohk = sb("ohk", [P, KB, D * HI], BF16)
        ohl = sb("ohl", [P, KB, P], BF16)
        ohd = sb("ohd", [P, 2, 4, D], BF16)
        tohd = sb("tohd", [P, 2, 4, NT], BF16)
        tohs = sb("tohs", [P, NT])
        spare = sb("spare", [P, 1])
        mm = sb("mm", [P, 2, 3])
        md = sb("md", [P, 2, 4])
        cb = sb("cb", [NT, 2, 4 * D])
        wm = sb("wm", [P, H])
        em = sb("em", [NT, H])
        bmb = sb("bmb", [NT, H])
        wih = sb("wih", [P, 3 * H])
        whh = sb("whh", [P, 3 * H])
        bi = sb("bi", [P, 3])
        bh = sb("bh", [P, 3])
        bs = sb("bs", [P, 2])
        eps = sb("eps", [P, 1])
        xb = sb("xb", [P, 2, BN])
        arena = sb("arena", [P, 8 * BN])
        temps = [arena[:, 0:6 * BN], mem[:, 0:6 * BN]]
        rzs = [a[:, 0:2 * BN].rearrange("p (a n) -> p a n", a=2) for a in temps]
        tns = [a[:, 2 * BN:5 * BN].rearrange("p (a n) -> p a n", a=3) for a in temps]
        yTs = [a[:, 5 * BN:6 * BN] for a in temps]
        yo = arena[:, 6 * BN:8 * BN].rearrange("p (a s h) -> p a s h", a=2, s=2)
        gm = arena[:, 0:2 * GP].rearrange("p (a g) -> p a g", a=2)
        dm = arena[:, 768:768 + 2 * DP].rearrange("p (a g) -> p a g", a=2)
        dI = ohk[:, :, :].rearrange("p k n -> p (k n)")[:, 0:2 * DP].bitcast(I32).rearrange("p (j e) -> p j e", j=4)
        st = sb("st", [P, 2, 6])
        mv = sb("mv", [P, 2, 2])
        rs = sb("rs", [P, 2])
        sd = sb("sd", [P, 2])

        x_d = nc.dram_tensor("x_split", (N, 3 * H), BF16, kind="Internal").ap()
        g_d = nc.dram_tensor("g_scratch", (2 * GP,), F32, kind="Internal").ap()
        d_d = nc.dram_tensor("d_scratch", (2 * DP,), F32, kind="Internal").ap()

        psb = pb("psb", [P, NB, 512])
        psf = pb("psf", [P, 512])
        psg = pb("psg", [P, 512])
        pA = pb("pA", [P, 512])
        pB = pb("pB", [P, 512])
        pC = pb("pC", [P, 512])
        xbank = [pA[:, :], pB[:, :], pC[:, :], psf[:, :]]
        banks = [(pA[:, :], pB[:, :], pC[:, :]), (psb[:, 0, :], psb[:, 1, :], psb[:, 2, :])]
        g2 = psg[:, 0:2 * W].rearrange("p (a w) -> p a w", a=2)
        g2s = psg[:, 0:2 * P].rearrange("p (a w) -> p a w", a=2)

        names = ("s_idx s_gl s_dl s_dt s_tl s_lb s_w s_io s_id s_d s_mg s_md s_sg s_sd2 s_bg s_bd2 s_fl "
                 "s_used s_oh s_grp s_acc s_ok  s_kd s_bd s_eb s_fd s_toh s_tr s_sl s_main "
                 "s_pm s_ms s_hh s_pg s_rz s_t2 s_n s_y s_pt s_mv s_sd s_ln s_xc s_p1 s_xe s_p2 s_xl s_xw s_nid").split()
        S = {n: sem(n) for n in names}
        s_g = [sem(f"s_g{i}") for i in range(RING)]
        s_xd = [sem(f"s_xd{i}") for i in range(4)]
        s_x = [sem(f"s_x{i}") for i in range(2)]
        s_o = [sem(f"s_o{i}") for i in range(2)]

        def xg32(slot):
            return xg[:, slot, 0:2 * H].bitcast(F32)

        def onehots(g):
            w = WG[g]
            f = ohs[:, g % AHEAD, 0:G * w]
            halves = f.bitcast(BF16).rearrange("p (g w k) -> p g w k", g=G, k=2)
            return f.rearrange("p (g w) -> p g w", g=G), halves[:, :, :, 1]

        def unit(u):
            return u * XU, min((u + 1) * XU, HI)

        def size(b):
            n = min(BN, N - b * BN)
            return b * BN, n, n // 2

        def read_flag(engine):
            return nc.values_load(flag[0:1, 0:1], engines=[engine], min_val=0, max_val=4 * GP,
                                  skip_runtime_bounds_check_because="a count of violated conditions")

        def store(sp, i):
            n0, n, q = size(ORDER[i])
            sp.wait_ge(S["s_ln"], i + 1)
            sp.dma_start(out[n0:n0 + n, :].rearrange("(p s) h -> p (s h)", s=2),
                         yo[0:q, i % 2, :, :].rearrange("p s h -> p (s h)")).then_inc(s_o[i % 2], 16)

        block = ctx.enter_context(nc.Block())

        @block.sync
        def _(sp):
            sp.dma_start(gI[:, :, :], dstG).then_inc(S["s_gl"], 16)
            sp.dma_start(dstI, dstT).then_inc(S["s_dt"], 16)
            sp.dma_start(typI, typT).then_inc(S["s_tl"], 16)
            sp.dma_start(lbF, low).then_inc(S["s_lb"], 16)

            def load_x(u):
                if u >= 4:
                    sp.wait_ge(S["s_p1"], u - 3)
                h0, h1 = unit(u)
                full = min(h1, HI - 1)
                sp.dma_start(x1[:, u % 4, 0:(full - h0) * H].rearrange("p (h f) -> p h f", f=H),
                             x[h0 * P:full * P, :].rearrange("(h p) f -> p h f", p=P)).then_inc(s_xd[u % 4], 16)
                if full < h1:
                    sp.dma_start(x1[0:TAIL, u % 4, (full - h0) * H:(h1 - h0) * H],
                                 x[full * P:N, :]).then_inc(s_xd[u % 4], 16)

            for u in range(4):
                load_x(u)
            sp.wait_ge(S["s_mg"], 1)
            sp.dma_start(g_d.rearrange("(a p j) -> p a j", a=2, j=3), mm[:, :, :]).then_inc(S["s_sg"], 16)
            sp.wait_ge(S["s_sg"], 16)
            sp.dma_start(gm.rearrange("p a g -> p (a g)"), g_d.partition_broadcast(P)).then_inc(S["s_bg"], 16)
            sp.wait_ge(S["s_md"], 1)
            sp.dma_start(d_d.rearrange("(a p j) -> p a j", a=2, j=4), md[:, :, :]).then_inc(S["s_sd2"], 16)
            sp.wait_ge(S["s_sd2"], 16)
            sp.dma_start(dm.rearrange("p a g -> p (a g)"), d_d.partition_broadcast(P)).then_inc(S["s_bd2"], 16)
            for u in range(4, PRE):
                load_x(u)
            sp.wait_ge(S["s_fl"], 1)
            bad = read_flag(ET.SP)

            def split_out(u):
                h0, h1 = unit(u)
                full = min(h1, HI - 1)
                sp.wait_ge(S["s_xl"], u + 1)
                sp.dma_start(x_d[h0 * P:full * P, :].rearrange("(h p) f -> p h f", p=P),
                             xs[:, h0:full, :, :].rearrange("p h c f -> p h (c f)")).then_inc(S["s_xw"], 16)
                if full < h1:
                    sp.dma_start(x_d[full * P:N, :],
                                 xs[0:TAIL, full, :, :].rearrange("p c f -> p (c f)")).then_inc(S["s_xw"], 16)

            with sp.If(bad == 0):
                for u in range(UNITS + 5):
                    if PRE <= u < UNITS:
                        load_x(u)
                    if u >= 5:
                        split_out(u - 5)
            for i, b in enumerate(ORDER):
                n0, n, q = size(b)
                if i >= 2:
                    sp.wait_ge(S["s_y"], i - 1)
                sp.dma_start(xb[:, i % 2, 0:n], xT[:, n0:n0 + n]).then_inc(s_x[i % 2], 16)
                if i >= 2:
                    store(sp, i - 2)
            for i in range(NBLK - 2, NBLK):
                store(sp, i)
            for j in range(2):
                sp.wait_ge(s_o[j], 16 * len(ORDER[j::2]))

        @block.gpsimd
        def _(pool):
            pool.iota(iota[:, :], [[1, D * HI]], base=0, channel_multiplier=0,
                      allow_small_or_imprecise_dtypes=True).then_inc(S["s_io"], 1)
            pool.iota(iotaF[:, :], [[1, W]], base=0, channel_multiplier=0,
                      allow_small_or_imprecise_dtypes=True).then_inc(S["s_io"], 1)
            pool.memset(ident[:, :], 0.0).then_inc(S["s_id"], 1)
            pool.wait_ge(S["s_id"], 1)
            pool.affine_select(out=ident[:, :], in_=ident[:, :], compare_op=ALU.not_equal, fill=1.0,
                               base=0, pattern=[[-1, P]], channel_multiplier=1).then_inc(S["s_id"], 1)
            pool.wait_ge(S["s_idx"], 16)

            def gather(p, split):
                if p >= RING:
                    pool.wait_ge(S["s_used"], p - RING + 1)
                pool.indirect_dma_start(
                    out=xg[:, p % RING, :] if split else xg32(p % RING), out_offset=None, in_=x_d if split else x,
                    in_offset=bass.IndirectOffsetOnAxis(ap=idx[:, p:p + 1], axis=0),
                ).then_inc(s_g[p % RING], 16)

            for p in range(SWITCH * G):
                gather(p, False)
            pool.wait_ge(S["s_fl"], 1)
            bad = read_flag(ET.Pool)
            with pool.If(bad == 0):
                pool.wait_ge(S["s_xw"], 16 * (UNITS + 1))
                for p in range(SWITCH * G, NG):
                    gather(p, True)
            with pool.Else():
                for p in range(SWITCH * G, TILES):
                    gather(p, False)

        @block.vector
        def _(v):
            cnt = [0]

            def link(ins):
                cnt[0] += 1
                ins.then_inc(S["s_d"], 1)
                v.wait_ge(S["s_d"], cnt[0])

            def more(ins):
                cnt[0] += 1
                ins.then_inc(S["s_d"], 1)

            def settle():
                v.wait_ge(S["s_d"], cnt[0])

            v.wait_ge(S["s_id"], 2)
            v.tensor_scalar(nid[:, :], ident[:, :], -1.0, None, ALU.mult).then_inc(S["s_nid"], 1)
            v.wait_ge(S["s_gl"], 16)
            v.tensor_reduce(mm[:, 0, :], gI, AX, ALU.min)
            v.tensor_reduce(mm[:, 1, :], gI, AX, ALU.max).then_inc(S["s_mg"], 1)
            v.wait_ge(S["s_dl"], 16)
            v.tensor_reduce(md[:, 0, :], dI, AX, ALU.min)
            v.tensor_reduce(md[:, 1, :], dI, AX, ALU.max).then_inc(S["s_md"], 1)
            more(v.memset(den[:, :, :], 0.0))
            more(v.memset(ring[:, :, 0:Z0 * BN], 0.0))
            more(v.memset(ring[:, :, R:R + W], 0.0))
            more(v.memset(psg[:, 0:2 * P], 0.0))
            more(v.memset(eps[:, :], EPS))
            v.wait_ge(S["s_tl"], 16)
            more(v.tensor_copy(typ[:, :], typI))
            v.wait_ge(S["s_dt"], 16)
            v.wait_ge(S["s_bg"], 16)
            more(v.tensor_tensor(rel[:, :, :], dstI[:, 0:NG].rearrange("p (g t) -> p g t", t=G),
                                 gm[:, 0, 0:GROUPS].unsqueeze(2).to_broadcast([P, GROUPS, G]), ALU.subtract))
            v.wait_ge(S["s_lb"], 16)
            g0 = gm[0:1, 0, 0:GROUPS]
            nd = len(DG)

            def part(t, k, n):
                return t[:, k * GROUPS:k * GROUPS + n]

            more(v.tensor_tensor(part(chk, 0, GROUPS), gm[0:1, 1, 0:GROUPS], g0, ALU.subtract))
            more(v.tensor_tensor(part(chk, 1, GROUPS), part(lbF, 0, GROUPS), g0, ALU.is_gt))
            more(v.tensor_tensor(part(chk, 2, GROUPS), part(lbF, 1, GROUPS), g0, ALU.is_lt))
            v.wait_ge(S["s_bd2"], 16)
            for j, t, k, n in runs():
                more(v.tensor_reduce(dbase[:, j:j + n],
                                     dm[:, 0, t:t + n * k].rearrange("p (n k) -> p n k", k=k), AX, ALU.min))
                more(v.tensor_reduce(dmax[:, j:j + n],
                                     dm[0:1, 1, t:t + n * k].rearrange("p (n k) -> p n k", k=k), AX, ALU.max))
            settle()
            c1, c2, c3 = (chk[:, 3 * GROUPS + k * nd:3 * GROUPS + (k + 1) * nd] for k in range(3))
            more(v.tensor_tensor(part(chk, 0, GROUPS), part(chk, 0, GROUPS), part(lbF, 2, GROUPS), ALU.is_ge))
            more(v.tensor_scalar(c1, dmax[:, :], float(DCAP), None, ALU.is_ge))
            more(v.tensor_tensor(c3, part(lbF, 3, nd), dbase[0:1, :], ALU.is_gt))
            link(v.tensor_tensor(c2, dmax[:, :], dbase[0:1, :], ALU.subtract))
            link(v.tensor_scalar(c2, c2, float(D), None, ALU.is_ge))
            link(v.tensor_reduce(vi[:, 0:1], chk, AX, ALU.add))
            v.tensor_copy(flag[:, :], vi[:, 0:1]).then_inc(S["s_fl"], 1)

            over = chk[:, 0:GROUPS]
            for _ in range((N - LOW0) // R):
                link(v.tensor_scalar(over, g0, float(LOW0 + R), float(R), ALU.is_ge, ALU.mult))
                link(v.tensor_tensor(g0, g0, over, ALU.subtract))
            more(v.tensor_scalar(gbI[:, :], g0, float(LOW0), None, ALU.subtract))
            v.wait_ge(S["s_w"], 16 * 7)
            more(v.tensor_tensor(em[:, :], em[:, :], bmb[:, :], ALU.add))
            link(v.tensor_tensor(bs[:, :], bi[:, 0:2], bh[:, 0:2], ALU.add))
            v.wait_ge(S["s_io"], 2)
            v.wait_ge(S["s_fl"], 1)
            bad = read_flag(ET.DVE)

            def final(kind, i, b, slow, seen):
                n0, n, q = size(b)
                k = wing(i, slow)
                _, pB, pC = banks[k]
                r = rzs[k][:, :, 0:n]
                yT = yTs[k]
                o = (n0 - LOW0) % R
                t = tns[k][:, :, 0:n]
                xx = xb[:, i % 2, 0:n]
                if kind == "t2":
                    v.wait_ge(S["s_rz"], 2 * i + 2)
                    v.wait_ge(S["s_pg"], i + 1)
                    link(v.scalar_tensor_tensor(out=t[:, 0, :], in0=pB[:, 0:n], scalar=bh[:, 2:3],
                                                in1=r[:, 0, :], op0=ALU.add, op1=ALU.mult))
                    v.tensor_tensor(t[:, 1, :], t[:, 0, :], pB[:, BN:BN + n], ALU.add).then_inc(S["s_t2"], 1)
                elif kind == "yt":
                    v.wait_ge(S["s_n"], i + 1)
                    more(v.tensor_tensor(t[:, 0, :], xx, t[:, 2, :], ALU.subtract))
                    more(v.tensor_tensor(t[:, 1, :], xx, t[:, 2, :], ALU.add))
                    v.wait_ge(S["s_d"], cnt[0] - 1)
                    link(v.tensor_tensor(t[:, 0, :], t[:, 0, :], r[:, 1, :], ALU.mult))
                    v.wait_ge(S["s_pg"], i + 1)
                    v.tensor_tensor(yT[:, 0:n], t[:, 0, :], t[:, 1, :], ALU.add).then_inc(S["s_y"], 1)
                elif kind == "bn":
                    v.wait_ge(S["s_pt"], i + 1)
                    for s in range(2):
                        more(v.bn_stats(st[0:q, s, :], pC[0:q, BN + s * H:BN + (s + 1) * H]))
                    for s in range(2):
                        v.wait_ge(S["s_d"], cnt[0] - 1 + s)
                        ins = v.bn_aggr(mv[0:q, s, :], st[0:q, s, :])
                    ins.then_inc(S["s_mv"], 1)
                elif kind == "ln":
                    v.wait_ge(S["s_sd"], i + 1)
                    if i >= 2:
                        v.wait_ge(s_o[i % 2], 16 * (i // 2))
                    link(v.reciprocal(rs[0:q, :], sd[0:q, :]))
                    for s in range(2):
                        ins = v.tensor_scalar(yo[0:q, i % 2, s, :], pC[0:q, BN + s * H:BN + (s + 1) * H],
                                              mv[0:q, s, 0:1], rs[0:q, s:s + 1], ALU.subtract, ALU.mult)
                    ins.then_inc(S["s_ln"], 1)
                    v.wait_ge(S["s_ln"], i + 1)
                elif kind == "zero":
                    v.wait_ge(S["s_pm"], i + 1)
                    v.wait_ge(S["s_acc"], seen)
                    v.memset(ring[:, :, o:o + n], 0.0).then_inc(S["s_acc"], 1)
            linked = cnt[0]
            with v.If(bad == 0):
                settle()
                regs = {}

                def prepare(it):
                    if it[0] == "G":
                        g = it[1]
                        b, w = g % AHEAD, WG[g]
                        if g >= AHEAD:
                            v.wait_ge(S["s_grp"], g - AHEAD + 1)
                        v.tensor_tensor(onehots(g)[0], rel[:, g, :].unsqueeze(2).to_broadcast([P, G, w]),
                                        iotaF[:, 0:w].unsqueeze(1).to_broadcast([P, G, w]), ALU.is_equal)
                        v.tensor_tensor(tohb[:, b, :, :],
                                        typ[:, g * G:g * G + G].unsqueeze(2).to_broadcast([P, G, NT]),
                                        iotaF[:, 0:NT].unsqueeze(1).to_broadcast([P, G, NT]),
                                        ALU.is_equal).then_inc(S["s_oh"], 1)
                    elif it[0] == "B":
                        _, j, e = it
                        b = e % KB
                        if e >= KB:
                            v.wait_ge(S["s_kd"], e - KB + 1)
                        if e % 4 == 0:
                            m = e // 4 % 2
                            v.tensor_tensor(ohd[:, m, :, :], dre[:, e:e + 4].unsqueeze(2).to_broadcast([P, 4, D]),
                                            iota[:, 0:D].unsqueeze(1).to_broadcast([P, 4, D]), ALU.is_equal)
                            v.tensor_tensor(tohd[:, m, :, :],
                                            typ[:, NG + e:NG + e + 4].unsqueeze(2).to_broadcast([P, 4, NT]),
                                            iota[:, 0:NT].unsqueeze(1).to_broadcast([P, 4, NT]), ALU.is_equal)
                        v.tensor_scalar(ohl[:, b, :], iota[:, 0:P], lo[:, e:e + 1], None, ALU.is_equal)
                        v.tensor_scalar(ohk[:, b, :], iota[:, :], key[:, e:e + 1], None,
                                        ALU.is_equal).then_inc(S["s_ok"], 1)

                def dense_keys():
                    v.wait_ge(S["s_idx"], 16)
                    more(v.tensor_scalar(hiI, idx[:, NG:TILES], 7, None, ALU.arith_shift_right))
                    more(v.tensor_scalar(loI, idx[:, NG:TILES], P - 1, None, ALU.bitwise_and))
                    more(v.tensor_copy(dbI[:, :], dbase[0:1, :]))
                    for j, t, k, n in runs():
                        more(v.tensor_tensor(dre[:, t:t + n * k].rearrange("p (n k) -> p n k", k=k),
                                             dstI[:, NG + t:NG + t + n * k].rearrange("p (n k) -> p n k", k=k),
                                             dbase[:, j:j + n].unsqueeze(2).to_broadcast([P, n, k]), ALU.subtract))
                    settle()
                    more(v.tensor_copy(lo[:, :], loI))
                    more(v.scalar_tensor_tensor(out=key[:, :], in0=dre[:, :], scalar=float(HI), in1=hiI,
                                                op0=ALU.mult, op1=ALU.add))
                    settle()

                def load_bases(table, at, k, hi):
                    _, vals = nc.values_load_multi_w_load_instructions(
                        table[0:1, at:at + k], engines=[ET.DVE], min_val=0, max_val=hi,
                        skip_runtime_bounds_check_because="the least destination of a group is a node")
                    return vals

                def consume(it):
                    seen = BEFORE[it]
                    if it[0] == "GA":
                        g = it[1]
                        if g % 4 == 0:
                            for j, q in enumerate(load_bases(gbI, g, min(4, GROUPS - g), R - 1)):
                                regs[g + j] = q
                        v.wait_ge(S["s_grp"], g + 1)
                        if seen:
                            v.wait_ge(S["s_acc"], seen)
                        d = ring[:, :, bass.ds(regs[g], WG[g])]
                        v.tensor_tensor(d, d, g2[:, :, 0:WG[g]], ALU.add).then_inc(S["s_acc"], 1)
                    elif it[0] == "dense":
                        dense_keys()
                    elif it[0] == "clear":
                        if it[1] == Z0:
                            v.wait_ge(S["s_p1"], UNITS)
                        o = it[1] * BN
                        v.memset(ring[:, :, o:o + BN], 0.0).then_inc(S["s_acc"], 1)
                    elif it[0] == "merge":
                        v.wait_ge(S["s_acc"], seen)
                        m = den[:, :, LOW0:DCAP]
                        v.tensor_tensor(m, m, ring[:, :, 0:DCAP - LOW0], ALU.add).then_inc(S["s_acc"], 1)
                        v.wait_ge(S["s_acc"], seen + 1)
                        v.memset(ring[:, :, 0:DCAP - LOW0], 0.0).then_inc(S["s_acc"], 1)
                    elif it[0] == "wrap":
                        v.wait_ge(S["s_acc"], seen)
                        m = ring[:, :, 0:W]
                        v.tensor_tensor(m, m, ring[:, :, R:R + W], ALU.add).then_inc(S["s_acc"], 1)
                        v.wait_ge(S["s_acc"], seen + 1)
                        v.memset(ring[:, :, R:R + W], 0.0).then_inc(S["s_acc"], 1)
                    elif it[0] == "A":
                        q = it[1]
                        bases = load_bases(dbI, 4 * q, 4, DCAP - 1)
                        v.wait_ge(S["s_fd"], q + 1)
                        for s in range(4):
                            v.wait_ge(S["s_acc"], seen + max(0, 2 * s - 1))
                            d = den[:, 0, bass.ds(bases[s], D)]
                            v.tensor_tensor(d, d, psf[:, s * D:(s + 1) * D], ALU.add).then_inc(S["s_acc"], 1)
                            if s:
                                v.wait_ge(S["s_acc"], seen + 2 * s)
                            c = den[0:NT, 1, bass.ds(bases[s], D)]
                            v.tensor_tensor(c, c, cb[:, q % 2, s * D:(s + 1) * D], ALU.add).then_inc(S["s_acc"], 1)
                    elif it[0] in STAGES or it[0] == "zero":
                        final(*it, False, seen)

                ahead = {None: [("G", 0)]}
                for kind, back in (("G", AHEAD - 1), ("B", KB - 1)):
                    own = [it for it in ITEMS if it[0] == kind]
                    for a, it in enumerate(own):
                        if it != ("G", 0):
                            ahead.setdefault((own[a - back] if kind == "B" else ("GA", own[a - back][1])) if a >= back
                                             else ("G", 0) if kind == "G" else ("dense",), []).append(it)
                for it in ahead[None]:
                    prepare(it)
                for it in ITEMS:
                    consume(it)
                    for nxt in ahead.get(it, []):
                        prepare(nxt)
            with v.Else():
                cnt[0] = linked
                settle()
                v.wait_ge(S["s_p1"], PRE)
                v.wait_ge(S["s_p2"], PRE - 1)
                v.wait_ge(S["s_xe"], PRE - 1)
                v.wait_ge(S["s_xl"], PRE - 2)
                link(v.memset(mem[:, 0:2 * ACC], 0.0))
                v.drain().then_inc(S["s_sl"], 1)
                with v.Fori(0, ROUNDS) as i:
                    for s in range(RING):
                        t = i * RING + s
                        v.wait_ge(S["s_tr"], t + 1)
                        v.tensor_tensor(tohs[:, :], typ[:, bass.ds(t, 1)].to_broadcast([P, NT]),
                                        iotaF[:, 0:NT], ALU.is_equal).then_inc(S["s_toh"], 1)
                        v.wait_ge(S["s_tr"], t + 2)
                        v.memset(spare[:, :], 0.0)
                        with v.Fori(0, P) as e:
                            d = nc.values_load(dstE[0:1, bass.ds(t * P + e, 1)], engines=[ET.DVE],
                                               min_val=0, max_val=DUMP,
                                               skip_runtime_bounds_check_because="a destination is a node")
                            q = whole[:, :, bass.ds(d, 1)]
                            v.tensor_tensor(q, q, g2s[:, :, bass.ds(e, 1)], ALU.add)
                            v.drain()
                        v.drain().then_inc(S["s_sl"], 1)
                v.drain().then_inc(S["s_main"], 1)
                for i, b in enumerate(ORDER):
                    for s in STAGES:
                        final(s, i, b, True, 0)

        @block.tensor
        def _(pe):
            def split(t):
                if t < UNITS:
                    h0, h1 = unit(t)
                    m = (h1 - h0) * H
                    pe.wait_ge(s_xd[t % 4], 16 * (t // 4 + 1) + (16 if h1 == HI else 0))
                    if t >= 4:
                        pe.wait_ge(S["s_xl"], t - 3)
                    pe.matmul(xbank[t % 4][:, 0:m], ident[:, :], x1[:, t % 4, 0:m], start=True, stop=True,
                              skip_group_check=True)
                    pe.wait_ge(S["s_xc"], t + 1)
                    pe.matmul(xbank[t % 4][:, 0:m], nid[:, :], xs[:, h0:h1, 0, :], start=False,
                              stop=True, skip_group_check=True).then_inc(S["s_p1"], 1)
                if 1 <= t <= UNITS:
                    h0, h1 = unit(t - 1)
                    m = (h1 - h0) * H
                    pe.wait_ge(S["s_xe"], t)
                    pe.matmul(xbank[(t - 1) % 4][:, 0:m], nid[:, :], xs[:, h0:h1, 1, :], start=False,
                              stop=True, skip_group_check=True).then_inc(S["s_p2"], 1)

            pe.wait_ge(S["s_id"], 2)
            pe.wait_ge(S["s_nid"], 1)
            for t in range(PRE):
                split(t)
            pe.wait_ge(S["s_fl"], 1)
            bad = read_flag(ET.PE)

            def final(kind, i, b, slow, seen):
                n0, n, q = size(b)
                xx = xb[:, i % 2, 0:n]
                w = wing(i, slow)
                p = before(i, slow)
                pA, pB, pC = banks[w]
                yT = yTs[w]
                if kind == "hh":
                    if slow:
                        pe.wait_ge(S["s_main"], 1)
                    else:
                        pe.wait_ge(S["s_acc"], seen)
                    o = (n0 - LOW0) % R
                    sums = whole[:, :, n0:n0 + n] if slow else \
                        den[:, :, n0:n0 + n] if b < CB0 else ring[:, :, o:o + n]
                    if p:
                        pe.wait_ge(S["s_ln"], p)
                    if i == 0 and not slow:
                        pe.wait_ge(S["s_xl"], UNITS)
                    if w and p == 0:
                        pe.wait_ge(S["s_eb"], 3 * len(DG))
                    pe.matmul(pC[:, 0:n], wm[:, :], sums[:, 0, :], start=True, stop=False,
                              skip_group_check=True)
                    pe.matmul(pC[:, 0:n], em[:, :], sums[0:NT, 1, :], start=False, stop=True,
                              skip_group_check=True).then_inc(S["s_pm"], 1)
                    pe.wait_ge(s_x[i % 2], 16 * (i // 2 + 1))
                    if p:
                        pe.wait_ge(S["s_rz"], 2 * p)
                        pe.wait_ge(S["s_t2"], p)
                    for k, (bank, o) in enumerate(((pA, 0), (pA, BN), (pB, 0))):
                        pe.matmul(bank[:, o:o + n], whh[:, k * H:(k + 1) * H], xx, start=(o == 0),
                                  stop=(k == 2), skip_group_check=True)
                elif kind == "ih":
                    pe.wait_ge(S["s_ms"], i + 1)
                    for k, (bank, o) in enumerate(((pA, 0), (pA, BN), (pB, BN))):
                        ins = pe.matmul(bank[:, o:o + n], wih[:, k * H:(k + 1) * H], yT[:, 0:n], start=False,
                                        stop=True, skip_group_check=True)
                    ins.then_inc(S["s_pg"], 1)
                elif kind == "turn":
                    pe.wait_ge(S["s_y"], i + 1)
                    yv = yT[:, 0:n].rearrange("f (p s) -> f s p", s=2)
                    for s in range(2):
                        ins = pe.transpose(pC[0:q, BN + s * H:BN + (s + 1) * H], yv[:, s, :], ident[:, :])
                    ins.then_inc(S["s_pt"], 1)

            with pe.If(bad == 0):
                pe.wait_ge(S["s_id"], 2)
                for it in ITEMS:
                    if it[0] == "G":
                        g = it[1]
                        w = WG[g]
                        oh, oh16 = onehots(g)
                        pe.wait_ge(S["s_oh"], g + 1)
                        if g:
                            pe.wait_ge(S["s_acc"], BEFORE[("GA", g - 1)] + 1)
                        for j in range(G):
                            p = g * G + j
                            pe.wait_ge(s_g[p % RING], 16 * (p // RING + 1))
                            if g < SWITCH:
                                ins = pe.matmul(g2[:, 0, 0:w], xg32(p % RING), oh[:, j, :], start=(j == 0),
                                                stop=(j == G - 1), skip_group_check=True)
                            else:
                                for c in range(3):
                                    ins = pe.matmul(g2[:, 0, 0:w], xg[:, p % RING, c * H:(c + 1) * H], oh16[:, j, :],
                                                    start=(j == 0 and c == 0), stop=(j == G - 1 and c == 2),
                                                    skip_group_check=True)
                            ins.then_inc(S["s_used"], 1)
                        for j in range(G):
                            ins = pe.matmul(g2[0:NT, 1, 0:w], tohb[:, g % AHEAD, j, :], oh16[:, j, :], start=False,
                                            stop=(j == G - 1), skip_group_check=True)
                        ins.then_inc(S["s_grp"], 1)
                    elif it[0] == "X":
                        split(it[1])
                    elif it[0] == "B":
                        _, j, e = it
                        t_j, k_j = DG[j]
                        first, last = e == t_j, e == t_j + k_j - 1
                        pe.wait_ge(S["s_ok"], e + 1)
                        b = e % KB
                        for i in range(NB):
                            if j and first:
                                pe.wait_ge(S["s_eb"], 3 * (j - 1) + i + 1)
                            pe.matmul(psb[:, i, 0:BC], ohl[:, b, :], ohk[:, b, i * BC:(i + 1) * BC],
                                      start=first, stop=last, skip_group_check=True)
                        pe.matmul(psb[0:NT, 0, BC:BC + D], tohd[:, e // 4 % 2, e % 4, :], ohd[:, e // 4 % 2, e % 4, :],
                                  start=False,
                                  stop=last, skip_group_check=True).then_inc(S["s_kd"], 1)
                    elif it[0] == "F":
                        _, q, f = it
                        if f == 0:
                            pe.wait_ge(S["s_eb"], 3 * (4 * q + 4))
                            if q == 0:
                                pe.wait_ge(S["s_xl"], UNITS)
                            else:
                                pe.wait_ge(S["s_acc"], BEFORE[("A", q - 1)] + 8)
                        for h in range(HI * f // PARTS, HI * (f + 1) // PARTS):
                            kk = P if h < HI - 1 else TAIL
                            for c in range(3):
                                ins = pe.matmul(psf[:, 0:4 * D], xs[0:kk, h, c, :], Bb[q % 2][0:kk, h, :],
                                                start=(h == 0 and c == 0), stop=(h == HI - 1 and c == 2),
                                                skip_group_check=True)
                        if f == PARTS - 1:
                            ins.then_inc(S["s_fd"], 1)
                    elif it[0] in STAGES:
                        final(*it, False, BEFORE[("sums", it[1])] if it[0] == "hh" else 0)
            with pe.Else():
                pe.wait_ge(S["s_id"], 2)
                pe.drain().then_inc(S["s_tr"], 1)
                with pe.Fori(0, ROUNDS) as i:
                    for s in range(RING):
                        t = i * RING + s
                        pe.wait_ge(s_g[s], (i + 1) * 16)
                        pe.wait_ge(S["s_toh"], t + 1)
                        pe.wait_ge(S["s_sl"], t + 1)
                        pe.transpose(g2s[:, 0, :], xg32(s), ident[:, :]).then_inc(S["s_used"], 1)
                        pe.transpose(g2s[0:NT, 1, :], tohs[:, :], ident[:, :]).then_inc(S["s_tr"], 1)
                for i, b in enumerate(ORDER):
                    for s in STAGES:
                        final(s, i, b, True, 0)

        @block.scalar
        def _(act):
            act.dma_start(idx[:, :], srcT).then_inc(S["s_idx"], 16)
            act.dma_start(dI, dstD).then_inc(S["s_dl"], 16)
            act.dma_start(wm[:, :], wmT).then_inc(S["s_w"], 16)
            act.dma_start(em[:, :], emb).then_inc(S["s_w"], 16)
            act.dma_start(bmb[:, :], bmsg.partition_broadcast(NT)).then_inc(S["s_w"], 16)
            act.dma_start(wih[:, :], wihT).then_inc(S["s_w"], 16)
            act.dma_start(whh[:, :], whhT).then_inc(S["s_w"], 16)
            act.dma_start(bi[:, :], bih).then_inc(S["s_w"], 16)
            act.dma_start(bh[:, :], bhh).then_inc(S["s_w"], 16)

            def split(t):
                if t < UNITS:
                    h0, h1 = unit(t)
                    act.wait_ge(s_xd[t % 4], 16 * (t // 4 + 1) + (16 if h1 == HI else 0))
                    act.copy(xs[:, h0:h1, 0, :], x1[:, t % 4, 0:(h1 - h0) * H].rearrange("p (h f) -> p h f", f=H)
                             ).then_inc(S["s_xc"], 1)
                for back, c, done, ready in ((1, 1, "s_xe", "s_p1"), (2, 2, "s_xl", "s_p2")):
                    if back <= t < UNITS + back:
                        h0, h1 = unit(t - back)
                        act.wait_ge(S[ready], t - back + 1)
                        act.copy(xs[:, h0:h1, c, :], xbank[(t - back) % 4][:, 0:(h1 - h0) * H]
                                 .rearrange("p (h f) -> p h f", f=H)).then_inc(S[done], 1)

            for t in range(PRE):
                split(t)
            act.wait_ge(S["s_fl"], 1)
            bad = read_flag(ET.Activation)

            def final(kind, i, b, slow):
                n0, n, q = size(b)
                w = wing(i, slow)
                p = before(i, slow)
                pA, _, pC = banks[w]
                rz, tn, msg = rzs[w], tns[w], yTs[w]
                if kind == "ms":
                    act.wait_ge(S["s_pm"], i + 1)
                    if p:
                        act.wait_ge(S["s_pt"], p)
                    if w and p == 0:
                        act.wait_ge(S["s_fd"], QUADS)
                    act.copy(msg[:, 0:n], pC[:, 0:n]).then_inc(S["s_ms"], 1)
                elif kind == "rz":
                    act.wait_ge(S["s_pg"], i + 1)
                    if p:
                        act.wait_ge(S["s_y"], p)
                    for k in range(2):
                        act.activation(rz[:, k, 0:n], pA[:, k * BN:k * BN + n], ACT.Sigmoid,
                                       bias=bs[:, k:k + 1]).then_inc(S["s_rz"], 1)
                elif kind == "th":
                    act.wait_ge(S["s_t2"], i + 1)
                    act.activation(tn[:, 2, 0:n], tn[:, 1, 0:n], ACT.Tanh, bias=bi[:, 2:3]).then_inc(S["s_n"], 1)
                elif kind == "sd":
                    act.wait_ge(S["s_mv"], i + 1)
                    if i:
                        act.wait_ge(S["s_ln"], i)
                    act.activation(sd[0:q, :], mv[0:q, :, 1], ACT.Sqrt, bias=eps[0:q, 0:1]).then_inc(S["s_sd"], 1)

            with act.If(bad == 0):
                for it in ITEMS:
                    if it[0] == "X":
                        split(it[1])
                    elif it[0] == "B":
                        _, j, e = it
                        if e == sum(DG[j]) - 1:
                            q, s = j // 4, j % 4
                            act.wait_ge(S["s_kd"], e + 1)
                            if s == 0 and q >= 2:
                                act.wait_ge(S["s_fd"], q - 1)
                                act.wait_ge(S["s_acc"], BEFORE[("A", q - 2)] + 8)
                            for i in range(NB):
                                o = s * D + i * DB
                                ins = act.copy(Bb[q % 2][:, :, o:o + DB].rearrange("p h d -> p d h"),
                                               psb[:, i, 0:BC].rearrange("p (d h) -> p d h", d=DB))
                                if i == 0:
                                    ins = act.copy(cb[:, q % 2, s * D:(s + 1) * D], psb[0:NT, 0, BC:BC + D])
                                ins.then_inc(S["s_eb"], 1)
                    elif it[0] in STAGES:
                        final(*it, False)
            with act.Else():
                for i, b in enumerate(ORDER):
                    for s in STAGES:
                        final(s, i, b, True)


def kernel(x, src, dst, edge_type_9, L0_gnn_W_msg, L0_gnn_b_msg, L0_gnn_edge_embed, L0_gnn_W_ih,
           L0_gnn_W_hh, L0_gnn_b_ih, L0_gnn_b_hh):
    import numpy as np
    import concourse.bacc as bacc
    from concourse.bass_utils import run_bass_kernel_spmd

    cut = T0 * P

    def lay(a):
        return np.ascontiguousarray(a)

    def turned(a, fill):
        a = np.asarray(a)
        return np.concatenate([a[cut:], np.full(EP - E, fill, a.dtype), a[:cut]])

    def by_tile(a, fill):
        return lay(turned(a, fill).reshape(TILES, P).T)

    def repeated(a, n):
        return np.concatenate([a, np.repeat(a[-1:], n - a.shape[0])])

    x, dst = np.asarray(x), np.asarray(dst)
    arrays = {
        "x": lay(x),
        "xT": lay(x.T),
        "srcT": by_tile(src, 0),
        "dstT": by_tile(dst, -1),
        "dstG": repeated(dst[cut:], GP * G * P).reshape(P, 3, G * P),
        "dstD": repeated(dst[:cut], DP * P).reshape(P, 4, P),
        "dstE": turned(dst, DUMP).reshape(1, EP),
        "typT": by_tile(edge_type_9, 0),
        "low": np.array([LB + UB + [float(w) for w in WG] + LBD], np.float32),
        "wmT": lay(np.asarray(L0_gnn_W_msg).T),
        "bmsg": lay(np.asarray(L0_gnn_b_msg)),
        "emb": lay(np.asarray(L0_gnn_edge_embed)),
        "wihT": lay(np.asarray(L0_gnn_W_ih).T),
        "whhT": lay(np.asarray(L0_gnn_W_hh).T),
        "bih": lay(np.asarray(L0_gnn_b_ih).reshape(3, H).T),
        "bhh": lay(np.asarray(L0_gnn_b_hh).reshape(3, H).T),
    }
    nc = bacc.Bacc("TRN2", target_bir_lowering=False, num_devices=1)
    args = [nc.dram_tensor(f"in_{k}", a.shape, mybir.dt.from_np(a.dtype), kind="ExternalInput").ap()
            for k, a in arrays.items()]
    out = nc.dram_tensor("out_0", (N, H), F32, kind="ExternalOutput").ap()
    gnn_kernel(nc, *args, out)
    r = run_bass_kernel_spmd(nc, [{f"in_{k}": a for k, a in arrays.items()}], core_ids=[0])
    return r.results[0]["out_0"]
```
